# Optimizing a Trainium2 kernel written in Bass

```python
import numpy as np
import jax
import jax.numpy as jnp

def _softmax(x, axis=-1):
    return jax.nn.softmax(x, axis=axis)

def _gelu(x):
    return jax.nn.gelu(x, approximate=True)

def _silu(x):
    return jax.nn.silu(x)

def _sigmoid(x):
    return jax.nn.sigmoid(x)

def _layernorm(x, axis=-1, eps=1e-05):
    m = jnp.mean(x, axis=axis, keepdims=True)
    v = jnp.var(x, axis=axis, keepdims=True)
    return (x - m) / jnp.sqrt(v + eps)

def _scatter_add(tgt, idx, src, axis=0):
    return tgt.at[idx].add(src)

def _segment_sum(src, seg, n):
    return jax.ops.segment_sum(src, seg, n)
kernel_name = 'mk_metaformer_d1_conv_nchw256_r2_3d605d'

def setup_inputs(seed: int=0):
    np.random.seed(seed)
    _w = jnp.asarray

    def _rec_inputs():
        import jax
        import jax.numpy as jnp
        _gk = jax.random.key(seed)
        x = -0.0002928 + 1 * jax.random.normal(jax.random.fold_in(_gk, 1), (16, 128, 32, 32), jnp.float32)
        return x
    x = _rec_inputs()

    def _L0_conv_setup():
        import jax, jax.numpy as jnp
        from jax import lax
        import numpy as np
        import math
        D_STATE = 2
        D_CONV = 4

        def _ln(x, g, b, eps=1e-05):
            m = x.mean(-1, keepdims=True)
            v = ((x - m) ** 2).mean(-1, keepdims=True)
            return (x - m) * lax.rsqrt(v + eps) * g + b

        def _mamba(x, Win, convw, convb, Wx, Wdt, bdt, Alog, Dp, Wout):
            b, L, dm = x.shape
            di = Win.shape[0] // 2
            n = Alog.shape[1]
            dtr = Wdt.shape[1]
            k = convw.shape[-1]
            xz = x @ Win.T
            xi, z = (xz[..., :di], xz[..., di:])
            xc = jnp.pad(xi, ((0, 0), (k - 1, 0), (0, 0))).transpose(0, 2, 1)
            xc = lax.conv_general_dilated(xc, convw, (1,), 'VALID', dimension_numbers=('NCH', 'OIH', 'NCH'), feature_group_count=di)
            xi = jax.nn.silu(xc.transpose(0, 2, 1) + convb)
            dbl = xi @ Wx.T
            dt = jax.nn.softplus(dbl[..., :dtr] @ Wdt.T + bdt)
            Bm = dbl[..., dtr:dtr + n]
            Cm = dbl[..., dtr + n:]
            A = -jnp.exp(Alog)
            dA = jnp.exp(dt[..., None] * A)
            dBx = dt[..., None] * Bm[:, :, None, :] * xi[..., None]

            def step(h, inp):
                dA_t, dBx_t, C_t = inp
                h = dA_t * h + dBx_t
                return (h, jnp.einsum('bdn,bn->bd', h, C_t))
            h0 = jnp.zeros((b, di, n), x.dtype)
            _, ys = lax.scan(step, h0, (dA.transpose(1, 0, 2, 3), dBx.transpose(1, 0, 2, 3), Cm.transpose(1, 0, 2)))
            y = ys.transpose(1, 0, 2) + Dp * xi
            y = y * jax.nn.silu(z)
            return y @ Wout.T
        key = jax.random.key(seed)
        ks = jax.random.split(key, 32)
        B, C, H, W = (16, 128, 32, 32)
        dm = H * W
        di = dm
        dtr = math.ceil(dm / 16)
        n, k = (D_STATE, D_CONV)

        def rn(i, shape, s):
            return (jax.random.normal(ks[i], shape) * s).astype(jnp.float32)
        inp = {'x': rn(0, (B, C, H, W), 1.0)}

        def mamba_p(pfx, base):
            inp[pfx + 'Win'] = rn(base, (2 * di, dm), dm ** (-0.5))
            inp[pfx + 'convw'] = rn(base + 1, (di, 1, k), k ** (-0.5))
            inp[pfx + 'convb'] = jnp.zeros((di,), jnp.float32)
            inp[pfx + 'Wx'] = rn(base + 2, (dtr + 2 * n, di), di ** (-0.5))
            inp[pfx + 'Wdt'] = rn(base + 3, (di, dtr), dtr ** (-0.5))
            inp[pfx + 'bdt'] = rn(base + 4, (di,), 0.1)
            inp[pfx + 'Alog'] = jnp.log(jnp.broadcast_to(jnp.arange(1, n + 1, dtype=jnp.float32), (di, n)))
            inp[pfx + 'D'] = jnp.ones((di,), jnp.float32)
            inp[pfx + 'Wout'] = rn(base + 5, (dm, di), di ** (-0.5))
        mamba_p('m1_', 1)
        mamba_p('m2_', 8)
        inp['ln1_g'] = jnp.ones((dm,), jnp.float32)
        inp['ln1_b'] = jnp.zeros((dm,), jnp.float32)
        inp['ln2_g'] = jnp.ones((dm,), jnp.float32)
        inp['ln2_b'] = jnp.zeros((dm,), jnp.float32)
        inp['W_mid'] = rn(15, (C, C), C ** (-0.5))
        inp['W_spa'] = rn(16, (dm, dm), dm ** (-0.5))
        inp['b_spa'] = jnp.zeros((dm,), jnp.float32)
        inp['W_res'] = rn(17, (C, C), C ** (-0.5))
        return inp
    _L0_conv_all = _L0_conv_setup()
    _L0_conv_in = {k: v for k, v in _L0_conv_all.items() if k in ('m1_Win', 'm1_convw', 'm1_convb', 'm1_Wx', 'm1_Wdt', 'm1_bdt', 'm1_Alog', 'm1_D', 'm1_Wout', 'm2_Win', 'm2_convw', 'm2_convb', 'm2_Wx', 'm2_Wdt', 'm2_bdt', 'm2_Alog', 'm2_D', 'm2_Wout', 'ln1_g', 'ln1_b', 'ln2_g', 'ln2_b', 'W_mid', 'W_spa', 'b_spa', 'W_res')}
    del _L0_conv_all

    def _L0_ffn_setup():
        import jax, jax.numpy as jnp
        import numpy as np
        B, N, D = (16, 2048, 128)
        NUM_EXPERTS, TOP_K, HEADS = (4, 2, 4)
        N_EDGES = 524288
        LN_EPS = 1e-05

        def _layernorm(x, g, b):
            mu = x.mean(-1, keepdims=True)
            var = ((x - mu) ** 2).mean(-1, keepdims=True)
            return (x - mu) * jax.lax.rsqrt(var + LN_EPS) * g + b

        def _forward(x, edge_index, W_gat, att_src, att_dst, b_gat, ln_gamma, ln_beta, W1, b1, W2, b2):
            Bc, Nc, Dc = x.shape
            M = Bc * Nc
            x_flat = x.reshape(M, Dc)
            h = (x_flat @ W_gat).reshape(M, HEADS, NUM_EXPERTS)
            loops = jnp.arange(M, dtype=edge_index.dtype)
            src = jnp.concatenate([edge_index[0], loops])
            dst = jnp.concatenate([edge_index[1], loops])
            a_src = (h * att_src).sum(-1)
            a_dst = (h * att_dst).sum(-1)
            e = jax.nn.leaky_relu(a_src[src] + a_dst[dst], negative_slope=0.2)
            e_max = jax.ops.segment_max(e, dst, num_segments=M)
            ee = jnp.exp(e - e_max[dst])
            denom = jax.ops.segment_sum(ee, dst, num_segments=M)
            alpha = ee / (denom[dst] + 1e-16)
            msg = h[src] * alpha[:, :, None]
            agg = jax.ops.segment_sum(msg, dst, num_segments=M).reshape(M, HEADS * NUM_EXPERTS) + b_gat
            scores = _layernorm(agg, ln_gamma, ln_beta).reshape(M, HEADS, NUM_EXPERTS).mean(1)
            scores = scores.reshape(Bc, Nc, NUM_EXPERTS)
            topk_s, topk_i = jax.lax.top_k(scores, TOP_K)
            w = jax.nn.softmax(topk_s, axis=-1)
            out = jnp.zeros_like(x)
            for ei in range(NUM_EXPERTS):
                g = jnp.where(topk_i == ei, w, 0.0).sum(-1)
                hh = jax.nn.gelu(x @ W1[ei] + b1[ei], approximate=False)
                out = out + g[..., None] * (hh @ W2[ei] + b2[ei])
            return out
        key = jax.random.key(seed)
        ks = jax.random.split(key, 8)
        s = 0.05
        return {'x': jax.random.normal(ks[0], (B, N, D), jnp.float32), 'W_gat': jax.random.normal(ks[1], (D, HEADS * NUM_EXPERTS), jnp.float32) * s, 'att_src': jax.random.normal(ks[2], (HEADS, NUM_EXPERTS), jnp.float32) * s, 'att_dst': jax.random.normal(ks[3], (HEADS, NUM_EXPERTS), jnp.float32) * s, 'b_gat': jnp.zeros((HEADS * NUM_EXPERTS,), jnp.float32), 'ln_gamma': jnp.ones((HEADS * NUM_EXPERTS,), jnp.float32), 'ln_beta': jnp.zeros((HEADS * NUM_EXPERTS,), jnp.float32), 'W1': jax.random.normal(ks[4], (NUM_EXPERTS, D, 2 * D), jnp.float32) * s, 'b1': jnp.zeros((NUM_EXPERTS, 2 * D), jnp.float32), 'W2': jax.random.normal(ks[5], (NUM_EXPERTS, 2 * D, D), jnp.float32) * s, 'b2': jnp.zeros((NUM_EXPERTS, D), jnp.float32), 'edge_index': jax.random.randint(ks[6], (2, N_EDGES), 0, B * N, jnp.int32)}
    _L0_ffn_all = _L0_ffn_setup()
    _L0_ffn_in = {k: v for k, v in _L0_ffn_all.items() if k in ('W_gat', 'att_src', 'att_dst', 'b_gat', 'ln_gamma', 'ln_beta', 'W1', 'b1', 'W2', 'b2', 'edge_index')}
    del _L0_ffn_all
    return {'x': x, 'L0_conv_m1_Win': _L0_conv_in['m1_Win'], 'L0_conv_m1_convw': _L0_conv_in['m1_convw'], 'L0_conv_m1_convb': _L0_conv_in['m1_convb'], 'L0_conv_m1_Wx': _L0_conv_in['m1_Wx'], 'L0_conv_m1_Wdt': _L0_conv_in['m1_Wdt'], 'L0_conv_m1_bdt': _L0_conv_in['m1_bdt'], 'L0_conv_m1_Alog': _L0_conv_in['m1_Alog'], 'L0_conv_m1_D': _L0_conv_in['m1_D'], 'L0_conv_m1_Wout': _L0_conv_in['m1_Wout'], 'L0_conv_m2_Win': _L0_conv_in['m2_Win'], 'L0_conv_m2_convw': _L0_conv_in['m2_convw'], 'L0_conv_m2_convb': _L0_conv_in['m2_convb'], 'L0_conv_m2_Wx': _L0_conv_in['m2_Wx'], 'L0_conv_m2_Wdt': _L0_conv_in['m2_Wdt'], 'L0_conv_m2_bdt': _L0_conv_in['m2_bdt'], 'L0_conv_m2_Alog': _L0_conv_in['m2_Alog'], 'L0_conv_m2_D': _L0_conv_in['m2_D'], 'L0_conv_m2_Wout': _L0_conv_in['m2_Wout'], 'L0_conv_ln1_g': _L0_conv_in['ln1_g'], 'L0_conv_ln1_b': _L0_conv_in['ln1_b'], 'L0_conv_ln2_g': _L0_conv_in['ln2_g'], 'L0_conv_ln2_b': _L0_conv_in['ln2_b'], 'L0_conv_W_mid': _L0_conv_in['W_mid'], 'L0_conv_W_spa': _L0_conv_in['W_spa'], 'L0_conv_b_spa': _L0_conv_in['b_spa'], 'L0_conv_W_res': _L0_conv_in['W_res'], 'L0_ffn_W_gat': _L0_ffn_in['W_gat'], 'L0_ffn_att_src': _L0_ffn_in['att_src'], 'L0_ffn_att_dst': _L0_ffn_in['att_dst'], 'L0_ffn_b_gat': _L0_ffn_in['b_gat'], 'L0_ffn_ln_gamma': _L0_ffn_in['ln_gamma'], 'L0_ffn_ln_beta': _L0_ffn_in['ln_beta'], 'L0_ffn_W1': _L0_ffn_in['W1'], 'L0_ffn_b1': _L0_ffn_in['b1'], 'L0_ffn_W2': _L0_ffn_in['W2'], 'L0_ffn_b2': _L0_ffn_in['b2'], 'L0_ffn_edge_index': _L0_ffn_in['edge_index']}

def reference(x, L0_conv_m1_Win, L0_conv_m1_convw, L0_conv_m1_convb, L0_conv_m1_Wx, L0_conv_m1_Wdt, L0_conv_m1_bdt, L0_conv_m1_Alog, L0_conv_m1_D, L0_conv_m1_Wout, L0_conv_m2_Win, L0_conv_m2_convw, L0_conv_m2_convb, L0_conv_m2_Wx, L0_conv_m2_Wdt, L0_conv_m2_bdt, L0_conv_m2_Alog, L0_conv_m2_D, L0_conv_m2_Wout, L0_conv_ln1_g, L0_conv_ln1_b, L0_conv_ln2_g, L0_conv_ln2_b, L0_conv_W_mid, L0_conv_W_spa, L0_conv_b_spa, L0_conv_W_res, L0_ffn_W_gat, L0_ffn_att_src, L0_ffn_att_dst, L0_ffn_b_gat, L0_ffn_ln_gamma, L0_ffn_ln_beta, L0_ffn_W1, L0_ffn_b1, L0_ffn_W2, L0_ffn_b2, L0_ffn_edge_index):
    import jax
    import jax.numpy as jnp

    def _L0_conv_ref(x, m1_Win, m1_convw, m1_convb, m1_Wx, m1_Wdt, m1_bdt, m1_Alog, m1_D, m1_Wout, m2_Win, m2_convw, m2_convb, m2_Wx, m2_Wdt, m2_bdt, m2_Alog, m2_D, m2_Wout, ln1_g, ln1_b, ln2_g, ln2_b, W_mid, W_spa, b_spa, W_res):
        import jax, jax.numpy as jnp
        from jax import lax
        import numpy as np
        import math
        D_STATE = 2
        D_CONV = 4

        def _ln(x, g, b, eps=1e-05):
            m = x.mean(-1, keepdims=True)
            v = ((x - m) ** 2).mean(-1, keepdims=True)
            return (x - m) * lax.rsqrt(v + eps) * g + b

        def _mamba(x, Win, convw, convb, Wx, Wdt, bdt, Alog, Dp, Wout):
            b, L, dm = x.shape
            di = Win.shape[0] // 2
            n = Alog.shape[1]
            dtr = Wdt.shape[1]
            k = convw.shape[-1]
            xz = x @ Win.T
            xi, z = (xz[..., :di], xz[..., di:])
            xc = jnp.pad(xi, ((0, 0), (k - 1, 0), (0, 0))).transpose(0, 2, 1)
            xc = lax.conv_general_dilated(xc, convw, (1,), 'VALID', dimension_numbers=('NCH', 'OIH', 'NCH'), feature_group_count=di)
            xi = jax.nn.silu(xc.transpose(0, 2, 1) + convb)
            dbl = xi @ Wx.T
            dt = jax.nn.softplus(dbl[..., :dtr] @ Wdt.T + bdt)
            Bm = dbl[..., dtr:dtr + n]
            Cm = dbl[..., dtr + n:]
            A = -jnp.exp(Alog)
            dA = jnp.exp(dt[..., None] * A)
            dBx = dt[..., None] * Bm[:, :, None, :] * xi[..., None]

            def step(h, inp):
                dA_t, dBx_t, C_t = inp
                h = dA_t * h + dBx_t
                return (h, jnp.einsum('bdn,bn->bd', h, C_t))
            h0 = jnp.zeros((b, di, n), x.dtype)
            _, ys = lax.scan(step, h0, (dA.transpose(1, 0, 2, 3), dBx.transpose(1, 0, 2, 3), Cm.transpose(1, 0, 2)))
            y = ys.transpose(1, 0, 2) + Dp * xi
            y = y * jax.nn.silu(z)
            return y @ Wout.T
        b, c, h, w = x.shape
        hw = h * w
        s = _mamba(x.reshape(b, c, hw), m1_Win, m1_convw, m1_convb, m1_Wx, m1_Wdt, m1_bdt, m1_Alog, m1_D, m1_Wout)
        s = _ln(s, ln1_g, ln1_b)
        s = jax.nn.silu(jnp.einsum('bcs,oc->bos', s, W_mid))
        s = _mamba(s, m2_Win, m2_convw, m2_convb, m2_Wx, m2_Wdt, m2_bdt, m2_Alog, m2_D, m2_Wout)
        s = _ln(s, ln2_g, ln2_b)
        r = jax.nn.silu(x.reshape(b, c, hw) @ W_spa.T + b_spa)
        r = jax.nn.silu(jnp.einsum('bcs,oc->bos', r, W_res))
        return jax.nn.silu(s + r).reshape(b, -1, h, w)

    def _L0_ffn_ref(x, W_gat, att_src, att_dst, b_gat, ln_gamma, ln_beta, W1, b1, W2, b2, edge_index):
        import jax, jax.numpy as jnp
        import numpy as np
        B, N, D = (16, 2048, 128)
        NUM_EXPERTS, TOP_K, HEADS = (4, 2, 4)
        N_EDGES = 524288
        LN_EPS = 1e-05

        def _layernorm(x, g, b):
            mu = x.mean(-1, keepdims=True)
            var = ((x - mu) ** 2).mean(-1, keepdims=True)
            return (x - mu) * jax.lax.rsqrt(var + LN_EPS) * g + b

        def _forward(x, edge_index, W_gat, att_src, att_dst, b_gat, ln_gamma, ln_beta, W1, b1, W2, b2):
            Bc, Nc, Dc = x.shape
            M = Bc * Nc
            x_flat = x.reshape(M, Dc)
            h = (x_flat @ W_gat).reshape(M, HEADS, NUM_EXPERTS)
            loops = jnp.arange(M, dtype=edge_index.dtype)
            src = jnp.concatenate([edge_index[0], loops])
            dst = jnp.concatenate([edge_index[1], loops])
            a_src = (h * att_src).sum(-1)
            a_dst = (h * att_dst).sum(-1)
            e = jax.nn.leaky_relu(a_src[src] + a_dst[dst], negative_slope=0.2)
            e_max = jax.ops.segment_max(e, dst, num_segments=M)
            ee = jnp.exp(e - e_max[dst])
            denom = jax.ops.segment_sum(ee, dst, num_segments=M)
            alpha = ee / (denom[dst] + 1e-16)
            msg = h[src] * alpha[:, :, None]
            agg = jax.ops.segment_sum(msg, dst, num_segments=M).reshape(M, HEADS * NUM_EXPERTS) + b_gat
            scores = _layernorm(agg, ln_gamma, ln_beta).reshape(M, HEADS, NUM_EXPERTS).mean(1)
            scores = scores.reshape(Bc, Nc, NUM_EXPERTS)
            topk_s, topk_i = jax.lax.top_k(scores, TOP_K)
            w = jax.nn.softmax(topk_s, axis=-1)
            out = jnp.zeros_like(x)
            for ei in range(NUM_EXPERTS):
                g = jnp.where(topk_i == ei, w, 0.0).sum(-1)
                hh = jax.nn.gelu(x @ W1[ei] + b1[ei], approximate=False)
                out = out + g[..., None] * (hh @ W2[ei] + b2[ei])
            return out
        return _forward(x, edge_index, W_gat, att_src, att_dst, b_gat, ln_gamma, ln_beta, W1, b1, W2, b2)

    def _gn(v, G=32, eps=1e-05):
        B_, C_, H_, W_ = v.shape
        g = v.reshape(B_, G, C_ // G, H_, W_)
        m = jnp.mean(g, axis=(2, 3, 4), keepdims=True)
        s = jnp.var(g, axis=(2, 3, 4), keepdims=True)
        return ((g - m) / jnp.sqrt(s + eps)).reshape(v.shape)

    def _ln_c(v, eps=1e-06):
        m = jnp.mean(v, axis=1, keepdims=True)
        s = jnp.var(v, axis=1, keepdims=True)
        return (v - m) / jnp.sqrt(s + eps)

    def _ln_t(v, eps=1e-05):
        m = jnp.mean(v, axis=-1, keepdims=True)
        s = jnp.var(v, axis=-1, keepdims=True)
        return (v - m) / jnp.sqrt(s + eps)

    def _to_tokens(v):
        B_, C_, H_, W_ = v.shape
        return v.reshape(B_, C_, H_ * W_).transpose(0, 2, 1)

    def _from_tokens(t, like):
        B_, C_, H_, W_ = like.shape
        return t.transpose(0, 2, 1).reshape(B_, C_, H_, W_)
    x = x + _L0_conv_ref(_ln_c(x), L0_conv_m1_Win, L0_conv_m1_convw, L0_conv_m1_convb, L0_conv_m1_Wx, L0_conv_m1_Wdt, L0_conv_m1_bdt, L0_conv_m1_Alog, L0_conv_m1_D, L0_conv_m1_Wout, L0_conv_m2_Win, L0_conv_m2_convw, L0_conv_m2_convb, L0_conv_m2_Wx, L0_conv_m2_Wdt, L0_conv_m2_bdt, L0_conv_m2_Alog, L0_conv_m2_D, L0_conv_m2_Wout, L0_conv_ln1_g, L0_conv_ln1_b, L0_conv_ln2_g, L0_conv_ln2_b, L0_conv_W_mid, L0_conv_W_spa, L0_conv_b_spa, L0_conv_W_res)
    t = _to_tokens(x)
    t = t + _L0_ffn_ref(_ln_t(t), L0_ffn_W_gat, L0_ffn_att_src, L0_ffn_att_dst, L0_ffn_b_gat, L0_ffn_ln_gamma, L0_ffn_ln_beta, L0_ffn_W1, L0_ffn_b1, L0_ffn_W2, L0_ffn_b2, L0_ffn_edge_index)
    x = _from_tokens(t, x)
    return x

_drawn_inputs = setup_inputs


def setup_inputs(seed=0):
    import zlib

    import numpy as np

    out = dict(_drawn_inputs(seed))
    spreads = {'L0_conv_m1_convb': (0.0, 0.1),
     'L0_conv_m1_D': (1.0, 0.2),
     'L0_conv_m2_convb': (0.0, 0.1),
     'L0_conv_m2_D': (1.0, 0.2),
     'L0_conv_ln1_g': (1.0, 0.2),
     'L0_conv_ln1_b': (0.0, 0.1),
     'L0_conv_ln2_g': (1.0, 0.2),
     'L0_conv_ln2_b': (0.0, 0.1),
     'L0_conv_b_spa': (0.0, 0.1),
     'L0_ffn_b_gat': (0.0, 0.1),
     'L0_ffn_ln_gamma': (1.0, 0.2),
     'L0_ffn_ln_beta': (0.0, 0.1),
     'L0_ffn_b1': (0.0, 0.292),
     'L0_ffn_b2': (0.0, 0.1)}
    factors = {'L0_conv_m2_bdt': 4.79, 'L0_ffn_att_src': 2.916, 'L0_ffn_att_dst': 4.015}
    for name, (base, spread) in spreads.items():
        noise = np.random.default_rng([zlib.crc32(name.encode()), seed]).standard_normal(out[name].shape)
        drawn = base * np.exp(spread * noise) if base else spread * noise
        out[name] = jnp.asarray(drawn.astype(out[name].dtype))
    for name, factor in factors.items():
        out[name] = (out[name] * factor).astype(out[name].dtype)
    return out
```

```python
from contextlib import ExitStack

import concourse.bass as bass
from concourse import mybir

ALU = mybir.AluOpType
ACT = mybir.ActivationFunctionType
AX = mybir.AxisListType
F32 = mybir.dt.float32
BF16 = mybir.dt.bfloat16
I32 = mybir.dt.int32

P = 128
B, C, S = 16, 128, 1024
NT = B * C
KC = S // P
DTR, NST, DCONV = 64, 2, 4
XD = DTR + 2 * NST
QW = 512
NQ = NT // QW
HALF = S // QW

M = B * S
NE = 524288
BINS = M // P
HEADS, EXP = 4, 4
CH = 8
QC = 4
QF = CH * QC
QUADS = NE // (P * QF)
EC = 4
CE = EC * P
CHUNKS = NE // CE + BINS + 8
SLOTS = CHUNKS * CE
SRC_BITS = 15
NO_NODE = M
EMPTY = (P << SRC_BITS) | NO_NODE
FAR = float(1 << 20)
BIG = 1e30
ROW = 32
FH = 2
D2 = 256

QUADS_P1 = 2
QUADS_P2 = 3
QUADS_OUT = 1


class Chain:

    def __init__(self, eng, sem, base=0):
        self.eng, self.sem, self.base, self.n = eng, sem, base, 0

    def mark(self, ins):
        self.n += 1
        ins.then_inc(self.sem, 1)
        return self.n

    def wait(self, mark):
        self.eng.wait_ge(self.sem, self.base + mark)

    def __call__(self, ins, wait_apart=None):
        self.n += 1
        ins.then_inc(self.sem, 1)
        if wait_apart:
            wait_apart(self.eng, (self.sem, self.base + self.n))
        else:
            self.eng.wait_ge(self.sem, self.base + self.n)

    def end(self, per):
        assert self.n == per, (self.n, per)


def program(nc, a, stop=99):
    ctx = ExitStack()
    scr = a["scratch"]

    def sem(name):
        return ctx.enter_context(nc.semaphore(name))

    with ctx:
        def sb(name, shape, dt, where=None):
            return (where or ctx).enter_context(nc.sbuf_tensor(name, shape, dt))

        def ps(name, shape, dt, where=None):
            return (where or ctx).enter_context(nc.psum_tensor(name, shape, dt))

        slots_d, counts_d, r_d, sz_d, tab_d = (scr[k] for k in ("slots", "counts", "r", "sz", "tab"))

        s_passed = sem("s_passed")

        def wait_apart(eng, *waits):
            for sem_, n in waits:
                eng.wait_ge(sem_, n)
            eng.sem_inc(s_passed, 1)

        ident = sb("ident", [P, P], F32)
        ident_b = sb("ident_b", [P, P], BF16)
        iota_b = sb("iota_b", [P, P], BF16)
        ones = sb("ones", [P, P], F32)
        inv_c = sb("inv_c", [P, P], F32)
        eps5 = sb("eps5", [P, 1], F32)
        eps6 = sb("eps6", [P, 1], F32)

        s_const = sem("s_const")
        s_dst = sem("s_dst")
        s_split = sem("s_split")
        s_hot = [sem("s_hot0"), sem("s_hot1")]
        s_hist = [sem("s_hist0"), sem("s_hist1")]
        s_histall = sem("s_histall")
        s_fill = sem("s_fill")
        s_ck = sem("s_ck")
        s_sv = sem("s_sv")
        s_sp = sem("s_sp")
        s_cnt = sem("s_cnt")
        s_cd = sem("s_cd")

        xT = sb("xT", [P, KC, NT], F32)
        act = sb("act", [P, KC, NT], F32)
        x2 = xT[:].rearrange("p k n -> p (k n)")
        tokens = act[:].rearrange("p k n -> p (k n)")

        estack = ctx.enter_context(ExitStack())
        upper = sb("upper", [P, P], BF16, estack)
        lower = sb("lower", [P, P], BF16, estack)
        hot = sb("hot", [P, QC, CH, P], BF16, estack)
        q_bin = sb("q_bin", [P, QF], I32, estack)
        q_binf = sb("q_binf", [P, QF], F32, estack)
        q_far = sb("q_far", [P, QF], F32, estack)
        q_lo = sb("q_lo", [P, QF], I32, estack)
        q_wrap = sb("q_wrap", [P, QF], F32, estack)
        q_srcf = sb("q_srcf", [P, QF], F32, estack)
        q_src = sb("q_src", [P, QF], I32, estack)
        q_pack = sb("q_pack", [P, QF], I32, estack)
        rank_f = sb("rank_f", [P, CH], F32, estack)
        prod = sb("prod", [P, CH, P], BF16, estack)
        slot_i = sb("slot_i", [P, QC, CH], I32, estack)
        pack_i = sb("pack_i", [P, QC, CH], I32, estack)

        bstack = ctx.enter_context(ExitStack())
        base_row = sb("base_row", [1, CH * P], F32, bstack)

        with ExitStack() as st:
            chunk_bin = sb("chunk_bin", [1, CHUNKS + 1], I32, st)
            NCOL = QUADS * QF
            dst = tokens[:, 0:NCOL].bitcast(I32).rearrange("p (q f) -> p q f", f=QF)
            tmp_i = tokens[:, NCOL:2 * NCOL].bitcast(I32)
            hi_a = x2[:, 0:NCOL].bitcast(BF16)[:, 0:NCOL]
            hi_b = x2[:, NCOL:2 * NCOL].bitcast(BF16)[:, 0:NCOL]
            hot_a = sb("hot_a", [P, 2, CH, 4, QC * 8], BF16, st)
            hot_b = sb("hot_b", [P, 2, P, 16], BF16, st)
            zero_b = sb("zero_b", [P, 256], BF16, st)
            fill = sb("fill", [P, SLOTS // P // 5], I32, st)
            part_i = sb("part_i", [P, 1], I32, st)
            part8 = sb("part8", [P, 1], I32, st)
            part8f = sb("part8f", [P, 1], F32, st)
            diag = sb("diag", [P, 16, 16], F32, st)
            col16 = sb("col16", [P, 16, 16], F32, st)
            masked = sb("masked", [P, 16, 16], F32, st)
            per_ab = sb("per_ab", [P, CH, 16], F32, st)
            sel_a = sb("sel_a", [P, 8], F32, st)
            cnt8 = sb("cnt8", [8, CH, 16], F32, st)
            cnt = sb("cnt", [1, CH, P], F32, st)
            tot = sb("tot", [1, P], F32, st)
            tot_i = sb("tot_i", [1, P], I32, st)
            nch_i = sb("nch_i", [1, P], I32, st)
            nch = sb("nch", [1, P], F32, st)
            ends = sb("ends", [1, P], F32, st)
            one_row = sb("one_row", [1, P], F32, st)
            ends_c = sb("ends_c", [P, 1], F32, st)
            chunk_no = sb("chunk_no", [P, CHUNKS], F32, st)
            past = sb("past", [P, CHUNKS], F32, st)
            cb_f = sb("cb_f", [1, CHUNKS], F32, st)
            round_i = sb("round_i", [1, 2], I32, st)
            ph = ps("ph", [P, CH, QW], F32, st)
            GROUPS = QUADS // 4

            with nc.Block() as block:
                @block.sync
                def _(sp):
                    sp.dma_start(dst, a["edges"][1].rearrange("(q p f) -> p q f", p=P, f=QF)).then_inc(s_dst, 16)
                    sp.wait_ge(s_const, 1)
                    for n in range(5):
                        w = SLOTS // 5
                        sp.dma_start(slots_d[n * w:(n + 1) * w, :].rearrange("(p f) o -> p (f o)", p=P),
                                     fill[:]).then_inc(s_fill, 16)
                    sp.wait_ge(s_cnt, 1)
                    for c in range(CH):
                        sp.dma_start(counts_d[c:c + 1, :].rearrange("o (h l) -> (o h) l", h=8),
                                     cnt8[:, c, :]).then_inc(s_cd, 16)
                    sp.wait_ge(s_cd, 16 * CH)
                    sp.dma_start(cnt[:].rearrange("o c b -> o (c b)"),
                                 counts_d[:, :].rearrange("(o c) b -> o (c b)", o=1)).then_inc(s_cd, 16)
                    sp.wait_ge(s_sv, 4)
                    sp.dma_start(scr["bins"], chunk_bin[:]).then_inc(s_fill, 16)
                    sp.wait_ge(s_fill, 96)

                @block.gpsimd
                def _(g):
                    g.memset(fill[:], EMPTY).then_inc(s_const, 1)
                    g.memset(ident[:], 0.0)
                    g.memset(ones[:], 1.0)
                    g.memset(inv_c[:], 1.0 / C)
                    g.memset(eps5[:], 1e-5)
                    g.memset(eps6[:], 1e-6)
                    g.memset(zero_b[:], 0.0)
                    g.memset(one_row[:], 1.0)
                    g.memset(upper[:], 1.0)
                    g.memset(lower[:], 1.0)
                    g.memset(hot[:], 0.0)
                    g.memset(sel_a[:], 0.0).then_inc(s_const, 1)
                    g.wait_ge(s_const, 2)
                    g.affine_select(out=ident[:], in_=ident[:], compare_op=ALU.not_equal, fill=1.0, base=0,
                                    pattern=[[-1, P]], channel_multiplier=1)
                    g.affine_select(out=upper[:], in_=upper[:], compare_op=ALU.is_ge, fill=0.0, base=-1,
                                    pattern=[[1, P]], channel_multiplier=-1)
                    g.affine_select(out=lower[:], in_=lower[:], compare_op=ALU.is_ge, fill=0.0, base=0,
                                    pattern=[[-1, P]], channel_multiplier=1)
                    g.iota(iota_b[:], pattern=[[1, P]], base=0, channel_multiplier=0,
                           allow_small_or_imprecise_dtypes=True)
                    g.iota(part_i[:], pattern=[[0, 1]], base=0, channel_multiplier=1)
                    g.iota(col16[:], pattern=[[1, 16], [0, 16]], base=0, channel_multiplier=0,
                           allow_small_or_imprecise_dtypes=True)
                    g.iota(chunk_no[:], pattern=[[1, CHUNKS]], base=0, channel_multiplier=0,
                           allow_small_or_imprecise_dtypes=True)
                    g.wait_ge(s_const, 2)
                    for k in range(16):
                        last = g.affine_select(out=sel_a[:], in_=sel_a[:], compare_op=ALU.not_equal, fill=1.0,
                                               base=-8 * k, pattern=[[-1, 8]], channel_multiplier=1)
                        last.then_inc(s_const, 1)
                        g.wait_ge(s_const, 3 + k)

                @block.vector
                def _(v):
                    ck = Chain(v, s_ck)
                    v.wait_ge(s_const, 18)
                    v.tensor_copy(ident_b[:], ident[:])
                    ck(v.tensor_scalar(part8[:], part_i[:], 3, None, ALU.logical_shift_right))
                    ck(v.tensor_copy(part8f[:], part8[:]))
                    ck(v.tensor_scalar(diag[:], col16[:], part8f[:, 0:1], None, ALU.is_equal))
                    v.wait_ge(s_dst, 16)
                    flat = dst.rearrange("p q f -> p (q f)")
                    ck(v.tensor_scalar(tmp_i, flat, 11, None, ALU.logical_shift_right))
                    ck(v.tensor_copy(hi_a, tmp_i))
                    ck(v.tensor_scalar(tmp_i, flat, 7, 15, ALU.logical_shift_right, ALU.bitwise_and))
                    ck(v.tensor_copy(hi_b, tmp_i))
                    with v.Fori(0, GROUPS // 2) as g:
                        for x in range(2):
                            v.wait_ge(s_hist[x], g)
                            fa = hi_a[:, bass.ds((2 * g + x) * P, P)]
                            fb = hi_b[:, bass.ds((2 * g + x) * P, P)]
                            for q in range(4):
                                v.tensor_tensor(hot_a[:, x, :, q, :].rearrange("p c (f a) -> p c f a", a=8),
                                                fa[:, q * QF:(q + 1) * QF].rearrange("p (c f) -> p c f", f=QC)
                                                .unsqueeze(3).to_broadcast([P, CH, QC, 8]),
                                                iota_b[:, 0:8].unsqueeze(1).unsqueeze(1)
                                                .to_broadcast([P, CH, QC, 8]), ALU.is_equal)
                            v.tensor_tensor(hot_b[:, x], fb.unsqueeze(2).to_broadcast([P, P, 16]),
                                            iota_b[:, 0:16].unsqueeze(1).to_broadcast([P, P, 16]),
                                            ALU.is_equal).then_inc(s_hot[x], 1)
                    v.wait_ge(s_hist[0], GROUPS // 2)
                    v.wait_ge(s_hist[1], GROUPS // 2)
                    for c in range(CH):
                        ck(v.tensor_tensor(masked[:], ph[:, c, 0:256].rearrange("p (a b) -> p a b", a=16),
                                           diag[:], ALU.mult))
                        ck(v.tensor_reduce(per_ab[:, c, :], masked[:].rearrange("p a b -> p b a"), AX.X, ALU.add))
                    v.sem_inc(s_sv, 1)
                    v.wait_ge(s_sp, 1)
                    v.tensor_copy(cnt8[:], ph[0:8, 0, 0:P].rearrange("p (c b) -> p c b", c=CH)).then_inc(s_cnt, 1)
                    v.wait_ge(s_cd, 16 * (CH + 1))
                    ck(v.tensor_reduce(tot[:], cnt[:].rearrange("o c b -> o b c"), AX.X, ALU.add))
                    ck(v.tensor_scalar(tot_i[:], tot[:], float(CE - 1), None, ALU.add))
                    ck(v.tensor_scalar(nch_i[:], tot_i[:], 9, None, ALU.logical_shift_right))
                    ck(v.tensor_copy(nch[:], nch_i[:]))
                    ck(v.tensor_tensor_scan(ends[:], one_row[:], nch[:], 0.0, ALU.mult, ALU.add))
                    ck(v.tensor_tensor(base_row[:, 0:P], ends[:], nch[:], ALU.subtract))
                    ck(v.tensor_scalar(base_row[:, 0:P], base_row[:, 0:P], float(CE), None, ALU.mult))
                    for c in range(1, CH):
                        ck(v.tensor_tensor(base_row[:, c * P:(c + 1) * P], base_row[:, (c - 1) * P:c * P],
                                           cnt[:, c - 1, :], ALU.add))
                    ck(v.tensor_scalar(round_i[:, 0:1], ends[:, P - 1:P], 3.0, 4.0, ALU.add, ALU.max))
                    ck(v.tensor_scalar(chunk_bin[:, CHUNKS:CHUNKS + 1], round_i[:, 0:1], 2, None,
                                       ALU.logical_shift_right))
                    v.sem_inc(s_sv, 1)
                    v.wait_ge(s_sp, 2)
                    ck(v.tensor_copy(ends_c[:], ph[:, 1, 0:1]))
                    ck(v.tensor_scalar(past[:], chunk_no[:], ends_c[:, 0:1], None, ALU.is_ge))
                    v.sem_inc(s_sv, 1)
                    v.wait_ge(s_sp, 3)
                    for n in range(0, CHUNKS, QW):
                        w = min(QW, CHUNKS - n)
                        ck(v.tensor_scalar(chunk_bin[:, n:n + w], ph[0:1, 2 + n // QW, 0:w], float(BINS - 1), None,
                                           ALU.min))
                    v.sem_inc(s_sv, 1)

                @block.tensor
                def _(t):
                    t.wait_ge(s_const, 18)
                    for c in range(CH):
                        t.matmul(ph[:, c, 0:256], zero_b[:, 0:P], zero_b[:], start=True, stop=True)
                    with t.Fori(0, GROUPS // 2) as g:
                        for x in range(2):
                            t.wait_ge(s_hot[x], g + 1)
                            for c in range(CH):
                                la = hot_a[:, x, c].rearrange("p q f -> p (q f)")
                                rb = hot_b[:, x].rearrange("p (q f) b -> p q (f b)", q=4)[:, :, c * 64:c * 64 + 64]
                                last = t.matmul(ph[:, c, 0:256].rearrange("p (q f) -> p q f", q=4), la, rb,
                                                start=False, stop=True, skip_group_check=True)
                            last.then_inc(s_hist[x], 1)
                    t.wait_ge(s_sv, 1)
                    t.matmul(ph[0:8, 0, 0:P], sel_a[:], per_ab[:].rearrange("p c b -> p (c b)"),
                             start=True, stop=True).then_inc(s_sp, 1)
                    t.wait_ge(s_sv, 2)
                    t.matmul(ph[:, 1, 0:1], ends[:], one_row[:, 0:1], start=True, stop=True).then_inc(s_sp, 1)
                    t.wait_ge(s_sv, 3)
                    for n in range(0, CHUNKS, QW):
                        w = min(QW, CHUNKS - n)
                        last = t.matmul(ph[0:1, 2 + n // QW, 0:w], ones[:, 0:1], past[:, n:n + w],
                                        start=True, stop=True)
                    last.then_inc(s_sp, 1)

        rank_ps = ps("rank_ps", [P, 2, 4, P], F32, estack)
        s_raw = sem("s_raw")
        s_eh = sem("s_eh")
        s_rank = [sem("s_rank0"), sem("s_rank1")]
        s_ttr = [sem("s_ttr0"), sem("s_ttr1")]
        s_slot = sem("s_slot")
        s_scat = [sem(f"s_scat{n}") for n in range(QC)]
        s_eck = sem("s_eck")
        EDGE_CK = 4

        edge_src = a["edges"][0].rearrange("(q p f) -> q p f", p=P, f=QF)
        edge_dst = a["edges"][1].rearrange("(q p f) -> q p f", p=P, f=QF)

        loads = [0]

        def edges_buffer(name, n, st):
            loads[0] += 1
            return sb("raw_" + name, [P, 2, n, QF], I32, st), loads[0]

        def edges_load(sp, raw, first, n):
            for i, edges in enumerate((edge_src, edge_dst)):
                sp.dma_start(raw[:, i, 0:n, :], edges[first:first + n].rearrange("q p f -> p q f")).then_inc(s_raw, 16)

        def edges_split(v, k, src, dst_):
            ck = Chain(v, s_eck, k * EDGE_CK)
            v.tensor_scalar(q_wrap[:], src, 0.0, float(M), ALU.is_lt, ALU.mult)
            v.tensor_scalar(q_lo[:], dst_, P - 1, SRC_BITS, ALU.bitwise_and, ALU.logical_shift_left)
            ck(v.tensor_scalar(q_bin[:], dst_, 7, None, ALU.logical_shift_right))
            v.tensor_copy(q_binf[:], q_bin[:])
            ck(v.tensor_tensor(q_srcf[:], src, q_wrap[:], ALU.add))
            v.tensor_scalar(q_far[:], q_binf[:], float(BINS), FAR, ALU.is_ge, ALU.mult)
            ck(v.tensor_scalar(q_src[:], q_srcf[:], float(M - 1), 0.0, ALU.min, ALU.max))
            ck(v.tensor_tensor(q_pack[:], q_src[:], q_lo[:], ALU.bitwise_or))
            ck.end(EDGE_CK)

        def edges_hot(v, t):
            v.tensor_tensor(hot[:, t], iota_b[:].unsqueeze(1).to_broadcast([P, CH, P]),
                            q_binf[:].rearrange("p (c t) -> p t c", t=QC)[:, t, :].unsqueeze(2)
                            .to_broadcast([P, CH, P]), ALU.is_equal).then_inc(s_eh, 1)

        def edges_vector(v, k, t, raw=None, at=None):
            v.wait_ge(s_slot, QC * k + t)
            for x in range(2):
                v.wait_ge(s_rank[x], QC * k + t + 1)
                for c in range(4):
                    last = v.tensor_tensor_reduce(prod[:, 4 * x + c], hot[:, t, 4 * x + c, :],
                                                  rank_ps[:, x, c, :], 1.0, 0.0, ALU.mult, ALU.add,
                                                  rank_f[:, 4 * x + c:4 * x + c + 1])
                last.then_inc(s_ttr[x], 1)
            if t + 1 < QC:
                edges_hot(v, t + 1)
            v.wait_ge(s_ttr[0], QC * k + t + 1)
            v.wait_ge(s_ttr[1], QC * k + t + 1)
            v.wait_ge(s_scat[t], 16 * CH * k)
            v.tensor_copy(pack_i[:, t, :], q_pack[:].rearrange("p (c t) -> p t c", t=QC)[:, t, :])
            v.tensor_tensor(slot_i[:, t, :], rank_f[:],
                            q_far[:].rearrange("p (c t) -> p t c", t=QC)[:, t, :],
                            ALU.add).then_inc(s_slot, 1)
            if t == QC - 1 and raw is not None:
                tile, load = raw
                v.wait_ge(s_raw, 32 * load)
                v.wait_ge(s_slot, QC * k + QC)
                edges_split(v, k + 1, *(tile[:, i, bass.ds(at, 1), :].rearrange("p o f -> p (o f)") for i in range(2)))
                edges_hot(v, 0)

        def edges_tensor(t_, k, t):
            t_.wait_ge(s_eh, QC * k + t + 1)
            for x in range(2):
                t_.wait_ge(s_ttr[x], QC * k + t)
                t_.matmul(rank_ps[:, x], lower[:], hot[:, (t - 1) % QC, 4 * x:4 * x + 4, :],
                          start=False, stop=True, skip_group_check=True)
                t_.matmul(rank_ps[:, x], upper[:], hot[:, t, 4 * x:4 * x + 4, :],
                          start=False, stop=True, skip_group_check=True).then_inc(s_rank[x], 1)

        def edges_gpsimd(g, first, n):
            with g.Fori(first, first + n) as k:
                for t in range(QC):
                    wait_apart(g, (s_slot, QC * k + t + 1))
                    for c in range(CH):
                        g.indirect_dma_start(slots_d[:, :], bass.IndirectOffsetOnAxis(ap=slot_i[:, t, c:c + 1], axis=0),
                                             pack_i[:, t, c:c + 1], None, bounds_check=SLOTS - 1,
                                             oob_is_err=False).then_inc(s_scat[t], 16)

        s_base = sem("s_base")
        with ExitStack() as st, nc.Block() as block:
            raw, load = edges_buffer("first", 1, st)

            @block.tensor
            def _(t):
                for x in range(2):
                    last = t.matmul(rank_ps[:, x], ones[0:1, :], base_row[:, x * QW:(x + 1) * QW],
                                    start=True, stop=True)
                last.then_inc(s_base, 1)
                t.wait_ge(s_base, 1)

            @block.sync
            def _(sp):
                edges_load(sp, raw, 0, 1)

            @block.vector
            def _(v):
                v.wait_ge(s_raw, 32)
                edges_split(v, 0, raw[:, 0, 0, :], raw[:, 1, 0, :])
                edges_hot(v, 0)
        bstack.close()

        mstack = ctx.enter_context(ExitStack())
        conv_ps = ps("conv_ps", [P, 6, QW], F32, mstack)
        big = sb("big", [P, 4, NT], F32, mstack)
        x_in = a["x"].rearrange("b c h w -> b c (h w)")

        s_px = sem("s_px")
        s_pw = sem("s_pw")
        s_pv = sem("s_pv")
        s_pa = sem("s_pa")
        s_pp = sem("s_pp")
        s_pr = sem("s_pr")
        with ExitStack() as st, nc.Block() as block:
            xin = sb("xin", [P, S], F32, st)
            xc = sb("xc", [P, S], F32, st)
            sq = sb("sq", [P, S], F32, st)
            xs = sb("xs", [P, KC, P], F32, st)
            r1 = sb("r1", [P, S], F32, st)
            r2 = sb("r2", [P, S], F32, st)
            b_spa = sb("b_spa", [1, S], F32, st)
            raw = edges_buffer("pre", B, st)
            w_res = sb("w_res", [P, P], F32, st)
            w_spa = act[:].rearrange("p k n -> p (k n)")[:, 0:KC * S].rearrange("p (k n) -> p k n", k=KC)
            pa, pb, pc = (conv_ps[:, 2 * n:2 * n + 2, :] for n in range(3))
            NV, NA, NP = 3, 6, 5

            def flat(t):
                return t.rearrange("p h n -> p (h n)")

            @block.sync
            def _(sp):
                edges_load(sp, raw[0], 1, B)
                sp.dma_start(w_spa, a["w_spaT"].rearrange("(k p) n -> p k n", p=P)).then_inc(s_pw, 16)
                sp.dma_start(b_spa[:], a["b_spa"].rearrange("(o n) -> o n", o=1)).then_inc(s_pw, 16)
                sp.dma_start(w_res[:], a["w_resT"]).then_inc(s_pw, 16)
                with sp.Fori(0, B) as b:
                    sp.wait_ge(s_pv, NV * b)
                    sp.dma_start(xin[:], x_in[bass.ds(b, 1)].rearrange("o c s -> (o c) s")).then_inc(s_px, 16)
                    sp.wait_ge(s_pa, NA * b + 6)
                    sp.dma_start(r_d[bass.ds(b, 1)].rearrange("o c s -> (o c) s"), r2[:]).then_inc(s_pr, 16)
                sp.wait_ge(s_pr, 16 * B)

            @block.vector
            def _(v):
                with v.Fori(0, B) as b:
                    v.wait_ge(s_px, 16 * b + 16)
                    v.wait_ge(s_pp, NP * b + 1)
                    v.wait_ge(s_pa, NA * b)
                    v.tensor_tensor(xc[:], xin[:], flat(pa), ALU.subtract).then_inc(s_pv, 1)
                    edges_vector(v, b, 0)
                    v.wait_ge(s_pa, NA * b + 2)
                    v.reciprocal(sq[:], sq[:]).then_inc(s_pv, 1)
                    v.wait_ge(s_pv, NV * b + 2)
                    v.tensor_tensor(xc[:], xc[:], sq[:], ALU.mult).then_inc(s_pv, 1)
                    for n in range(1, QC):
                        edges_vector(v, b, n, raw, b)

            @block.scalar
            def _(s):
                with s.Fori(0, B) as b:
                    s.wait_ge(s_pv, NV * b + 1)
                    s.activation(sq[:], xc[:], ACT.Square).then_inc(s_pa, 1)
                    s.wait_ge(s_pp, NP * b + 2)
                    s.wait_ge(s_pa, NA * b + 1)
                    s.activation(sq[:], flat(pb), ACT.Sqrt, bias=eps6[:, 0:1]).then_inc(s_pa, 1)
                    s.wait_ge(s_pp, NP * b + 3)
                    s.activation(xs[:], flat(pc).rearrange("p (k n) -> p k n", k=KC), ACT.Copy).then_inc(s_pa, 1)
                    s.activation(xT[:, :, bass.ds(b * P, P)], flat(pc).rearrange("p (k n) -> p k n", k=KC),
                                 ACT.Copy).then_inc(s_pa, 1)
                    s.wait_ge(s_pp, NP * b + 4)
                    s.activation(r1[:], flat(pa), ACT.Silu).then_inc(s_pa, 1)
                    s.wait_ge(s_pp, NP * b + 5)
                    s.wait_ge(s_pr, 16 * b)
                    s.activation(r2[:], flat(pb), ACT.Silu).then_inc(s_pa, 1)

            @block.tensor
            def _(t):
                t.wait_ge(s_pw, 48)
                with t.Fori(0, B) as b:
                    t.wait_ge(s_px, 16 * b + 16)
                    t.wait_ge(s_pa, NA * b)
                    for h in range(HALF):
                        last = t.matmul(pa[:, h], inv_c[:], xin[:, h * QW:(h + 1) * QW], start=True, stop=True)
                    last.then_inc(s_pp, 1)
                    edges_tensor(t, b, 0)
                    t.wait_ge(s_pa, NA * b + 1)
                    for h in range(HALF):
                        last = t.matmul(pb[:, h], inv_c[:], sq[:, h * QW:(h + 1) * QW], start=True, stop=True)
                    last.then_inc(s_pp, 1)
                    edges_tensor(t, b, 1)
                    t.wait_ge(s_pv, NV * b + 3)
                    for k in range(KC):
                        last = t.transpose(pc[:, k // 4, (k % 4) * P:(k % 4 + 1) * P], xc[:, k * P:(k + 1) * P],
                                           ident[:])
                    last.then_inc(s_pp, 1)
                    edges_tensor(t, b, 2)
                    t.wait_ge(s_pa, NA * b + 3)
                    for h in range(HALF):
                        for k in range(KC):
                            t.matmul(pa[:, h], xs[:, k, :], w_spa[:, k, h * QW:(h + 1) * QW],
                                     start=(k == 0), stop=False)
                        last = t.matmul(pa[:, h], ones[0:1, :], b_spa[:, h * QW:(h + 1) * QW], start=False, stop=True)
                    last.then_inc(s_pp, 1)
                    edges_tensor(t, b, 3)
                    t.wait_ge(s_pa, NA * b + 5)
                    for h in range(HALF):
                        last = t.matmul(pb[:, h], w_res[:], r1[:, h * QW:(h + 1) * QW], start=True, stop=True)
                    last.then_inc(s_pp, 1)

            @block.gpsimd
            def _(g):
                edges_gpsimd(g, 0, B)

        quads = B
        for m in (1, 2):
            w = {k: a[f"m{m}_{k}"] for k in ("WinT", "convw", "convb", "WxT", "WdtT", "bdt", "Alog", "D", "WoutT")}
            n = f"_{m}"
            lstack = ExitStack()
            layer_sems = []

            def sem_l(name):
                layer_sems.append(nc.alloc_semaphore(name=name))
                return layer_sems[-1]

            conv_w = sb("conv_w" + n, [P, KC, DCONV], F32, lstack)
            conv_b = sb("conv_b" + n, [P, KC], F32, lstack)
            dt_b = sb("dt_b" + n, [P, KC], F32, lstack)
            rate = sb("rate" + n, [P, KC, NST], F32, lstack)
            skip = sb("skip" + n, [P, KC], F32, lstack)
            s_small = sem_l("s_small" + n)

            s_w = [sem_l(f"s_w{x}{n}") for x in range(2)]
            s_jdone = [sem_l(f"s_jdone{x}{n}") for x in range(2)]
            s_mm = [sem_l(f"s_mm{x}{n}") for x in range(2)]
            s_ev = [sem_l(f"s_ev{x}{n}") for x in range(2)]
            s_zev = [sem_l(f"s_zev{x}{n}") for x in range(2)]
            s_cv = [sem_l(f"s_cv{x}{n}") for x in range(2)]
            s_cch = sem_l("s_cch" + n)
            s_pad = sem_l("s_pad" + n)
            s_u = sem_l("s_u" + n)
            s_zs = [sem_l(f"s_zs{x}{n}") for x in range(2)]
            s_rate = sem_l("s_rate" + n)
            with ExitStack() as st, nc.Block() as block:
                raw = edges_buffer("in" + n, KC * QUADS_P1, st)
                w_in = big[:].rearrange("p k n -> p (k n)")[:, 0:4 * S].rearrange(
                    "p (x z k n) -> p x z k n", x=2, z=2, k=KC)
                w_x = sb("w_x" + n, [P, 2, XD], F32, st)
                padded = [sb(f"padded{x}{n}", [P, 4, P + DCONV - 1], F32, st) for x in range(2)]
                acc = [sb(f"acc{x}{n}", [P, 4, P], F32, st) for x in range(2)]
                zst = [sb(f"zst{x}{n}", [P, QW], F32, st) for x in range(2)]
                bank = [conv_ps[:, 4, :], conv_ps[:, 5, :]]
                JJ = KC // 2

                @block.sync
                def _(sp):
                    edges_load(sp, raw[0], quads + 1, KC * QUADS_P1)
                    for dst_, src_ in ((conv_w[:], w["convw"].rearrange("(k p) o t -> p k (o t)", p=P)),
                                       (conv_b[:], w["convb"].rearrange("(k p) -> p k", p=P)),
                                       (dt_b[:], w["bdt"].rearrange("(k p) -> p k", p=P)),
                                       (rate[:], w["Alog"].rearrange("(k p) t -> p k t", p=P)),
                                       (skip[:], w["D"].rearrange("(k p) -> p k", p=P))):
                        with nc.allow_non_contiguous_dma(reason="small parameters, one to a partition"):
                            sp.dma_start(dst_, src_).then_inc(s_small, 16)
                    with sp.Fori(0, JJ) as jj:
                        for x in range(2):
                            j = 2 * jj + x
                            sp.wait_ge(s_jdone[x], jj)
                            for z in range(2):
                                sp.dma_start(w_in[:, x, z], w["WinT"].rearrange("(k p) n -> p k n", p=P)
                                             [:, :, bass.ds(j * P + z * S, P)]).then_inc(s_w[x], 16)
                            sp.dma_start(w_x[:, x], w["WxT"][bass.ds(j * P, P), :]).then_inc(s_w[x], 16)
                            for q in range(NQ):
                                sp.wait_ge(s_zev[q % 2], 4 * jj + 2 * x + q // 2 + 1)
                                sp.dma_start(sz_d[bass.ds(j, 1), :, q * QW:(q + 1) * QW]
                                             .rearrange("o p n -> (o p) n"), zst[q % 2][:]).then_inc(s_zs[q % 2], 16)
                    for x in range(2):
                        sp.wait_ge(s_zs[x], 16 * KC * 2)

                @block.vector
                def _(v):
                    for x in range(2):
                        v.memset(padded[x][:], 0.0).then_inc(s_pad, 1)
                    v.wait_ge(s_small, 80)
                    with v.Fori(0, KC) as j:
                        ck = Chain(v, s_cch, 8 * j)
                        for z in range(2):
                            for q in range(NQ):
                                edges_vector(v, quads + 2 * j + z, q, raw, 2 * j + z)
                                if z:
                                    continue
                                x = q % 2
                                v.wait_ge(s_ev[x], 2 * j + q // 2 + 1)
                                for tap in (2, 1, 0):
                                    op = v.scalar_tensor_tensor(
                                        out=acc[x][:], in0=padded[x][:, :, tap:tap + P],
                                        scalar=conv_w[:, bass.ds(j, 1), tap:tap + 1].rearrange("p k t -> p (k t)"),
                                        in1=acc[x][:], op0=ALU.mult, op1=ALU.add)
                                    if tap:
                                        ck(op)
                                    else:
                                        op.then_inc(s_cv[x], 1)
                        ck.end(8)

                @block.scalar
                def _(s):
                    s.wait_ge(s_pad, 2)
                    s.wait_ge(s_small, 80)
                    with s.Fori(0, KC) as j:
                        def evacuate(q):
                            x = q % 2
                            s.wait_ge(s_mm[x], 4 * j + q // 2 + 1)
                            s.wait_ge(s_cv[x], 2 * j + q // 2)
                            s.wait_ge(s_u, 4 * j + max(q - 1, 0))
                            src = bank[x].rearrange("p (b n) -> p b n", n=P)
                            s.activation(padded[x][:, :, DCONV - 1:], src, ACT.Copy)
                            s.activation(acc[x][:], src, ACT.Identity, bias=conv_b[:, bass.ds(j, 1)],
                                         scale=conv_w[:, bass.ds(j, 1), 3:4].rearrange("p k t -> p (k t)"))\
                                .then_inc(s_ev[x], 1)

                        def gate(q):
                            x = q % 2
                            wait_apart(s, (s_cv[x], 2 * j + q // 2 + 1))
                            s.activation(act[:, bass.ds(j, 1), q * QW:(q + 1) * QW],
                                         acc[x][:].rearrange("p b n -> p (b n)").unsqueeze(1),
                                         ACT.Silu).then_inc(s_u, 1)

                        evacuate(0)
                        for q in range(1, NQ):
                            evacuate(q)
                            gate(q - 1)
                        gate(NQ - 1)
                        for q in range(NQ):
                            x = q % 2
                            s.wait_ge(s_mm[x], 4 * j + 2 + q // 2 + 1)
                            s.wait_ge(s_zs[x], 32 * j + 16 * (q // 2))
                            s.activation(zst[x][:], bank[x], ACT.Silu).then_inc(s_zev[x], 1)
                    s.activation(rate[:], rate[:], ACT.Exp).then_inc(s_rate, 1)
                    s.wait_ge(s_rate, 1)
                    s.mul(rate[:], rate[:], -1.0).then_inc(s_rate, 1)

                @block.tensor
                def _(t):
                    t.wait_ge(s_pad, 2)
                    for q in range(NQ):
                        t.matmul(conv_ps[0:XD, q, :], padded[0][:, 0, 0:XD],
                                 padded[0][:].rearrange("p b n -> p (b n)")[:, 0:QW], start=True, stop=True)
                    with t.Fori(0, JJ) as jj:
                        for x_ in range(2):
                            t.wait_ge(s_w[x_], 48 * jj + 48)
                            for z in range(2):
                                for q in range(NQ):
                                    x = q % 2
                                    if z == 0 and q < 2:
                                        t.wait_ge(s_zev[x], 4 * jj + 2 * x_)
                                    elif z == 0:
                                        t.wait_ge(s_ev[x], 4 * jj + 2 * x_ + 1)
                                    elif q < 2:
                                        t.wait_ge(s_ev[x], 4 * jj + 2 * x_ + 2)
                                    else:
                                        t.wait_ge(s_zev[x], 4 * jj + 2 * x_ + 1)
                                    for k in range(KC):
                                        last = t.matmul(bank[x], w_in[:, x_, z, k, :],
                                                        xT[:, k, q * QW:(q + 1) * QW],
                                                        start=(k == 0), stop=(k == KC - 1))
                                    last.then_inc(s_mm[x], 1)
                                    edges_tensor(t, quads + 2 * (2 * jj + x_) + z, q)
                            for q in range(NQ):
                                t.wait_ge(s_u, 8 * jj + 4 * x_ + q + 1)
                                last = t.matmul(conv_ps[0:XD, q, :], w_x[:, x_, :],
                                                act[:, bass.ds(2 * jj + x_, 1), q * QW:(q + 1) * QW],
                                                start=False, stop=True, skip_group_check=True)
                            last.then_inc(s_jdone[x_], 1)

                @block.gpsimd
                def _(g):
                    edges_gpsimd(g, quads, KC * QUADS_P1)
            quads += KC * QUADS_P1

            s_dbl = sem_l("s_dbl" + n)
            s_sp2 = sem_l("s_spread" + n)
            s_spev = sem_l("s_spev" + n)
            s_wdt = [sem_l(f"s_wdt{x}{n}") for x in range(2)]
            s_dtmm = [sem_l(f"s_dtmm{x}{n}") for x in range(2)]
            s_soft = [sem_l(f"s_soft{x}{n}") for x in range(2)]
            s_ach = sem_l("s_ach" + n)
            s_dt = [sem_l(f"s_dt{x}{n}") for x in range(2)]
            s_decay = [sem_l(f"s_decay{x}{n}") for x in range(2)]
            s_gz = [sem_l(f"s_gz{x}{n}") for x in range(2)]
            s_y = [sem_l(f"s_y{x}{n}") for x in range(2)]
            s_vch = sem_l("s_vch" + n)
            with ExitStack() as st, nc.Block() as block:
                dbl = sb("dbl" + n, [XD, NT], F32, st)
                raw = edges_buffer("scan" + n, KC * QUADS_P2, st)
                w_dt = sb("w_dt" + n, [DTR, 2, P], F32, st)
                free = xT[:].rearrange("p k (c n) -> p (k c) n", n=QW)
                soft, relu, dec0, dec1, gz, dtu, h0, h1 = ([free[:, 2 * i + x, :] for x in range(2)] for i in range(8))
                bank = [conv_ps[:, 4, :], conv_ps[:, 5, :]]
                JJ = KC // 2

                @block.sync
                def _(sp):
                    edges_load(sp, raw[0], quads + 1, KC * QUADS_P2)
                    with sp.Fori(0, JJ) as jj:
                        for x_ in range(2):
                            j = 2 * jj + x_
                            for q in range(NQ):
                                x = q % 2
                                sp.wait_ge(s_y[x], 4 * jj + 2 * x_ + q // 2)
                                if q == 1:
                                    sp.dma_start(w_dt[:, x_], w["WdtT"][:, bass.ds(j * P, P)]).then_inc(s_wdt[x_], 16)
                                sp.dma_start(gz[x], sz_d[bass.ds(j, 1), :, q * QW:(q + 1) * QW]
                                             .rearrange("o p n -> (o p) n")).then_inc(s_gz[x], 16)

                @block.tensor
                def _(t):
                    t.wait_ge(s_dbl, 1)
                    for r in range(2 * NST):
                        for q in range(NQ):
                            i = r * NQ + q
                            if i >= 2:
                                t.wait_ge(s_spev, i - 1)
                            t.matmul(bank[i % 2], ident[0:XD, DTR + r:DTR + r + 1].to_broadcast([XD, P]),
                                     dbl[:, q * QW:(q + 1) * QW], start=True, stop=True).then_inc(s_sp2, 1)
                    t.wait_ge(s_spev, 4 * NQ)
                    with t.Fori(0, JJ) as jj:
                        for x_ in range(2):
                            t.wait_ge(s_wdt[x_], 16 * jj + 16)

                            def dt_product(q):
                                x = q % 2
                                t.wait_ge(s_soft[x], 4 * jj + 2 * x_ + q // 2)
                                t.matmul(bank[x], w_dt[:, x_, :], dbl[0:DTR, q * QW:(q + 1) * QW],
                                         start=True, stop=True).then_inc(s_dtmm[x], 1)

                            dt_product(0)
                            for q in range(NQ):
                                if q + 1 < NQ:
                                    dt_product(q + 1)
                                for e in range(QUADS_P2 * q, QUADS_P2 * (q + 1)):
                                    edges_tensor(t, quads + (2 * jj + x_) * QUADS_P2 + e // QC, e % QC)

                @block.scalar
                def _(s):
                    s.activation(dbl[:].rearrange("p (q n) -> p q n", q=NQ), conv_ps[0:XD, 0:NQ, :],
                                 ACT.Copy).then_inc(s_dbl, 1)
                    for i in range(2 * NST * NQ):
                        s.wait_ge(s_sp2, i + 1)
                        s.activation(big[:, i // NQ, (i % NQ) * QW:(i % NQ + 1) * QW], bank[i % 2],
                                     ACT.Copy).then_inc(s_spev, 1)
                    with s.Fori(0, KC) as j:
                        ck = Chain(s, s_ach, 2 * NQ * j)

                        def softplus(q):
                            x = q % 2
                            wait_apart(s, (s_dtmm[x], 2 * j + q // 2 + 1), (s_y[x], 2 * j + q // 2))
                            bias = dt_b[:, bass.ds(j, 1)]
                            s.activation(relu[x], bank[x], ACT.Relu, bias=bias)
                            ck(s.activation(soft[x], bank[x], ACT.Abs, bias=bias))
                            ck(s.activation(soft[x], soft[x], ACT.Exp, scale=-1.0))
                            s.activation(soft[x], soft[x], ACT.Ln, bias=1.0).then_inc(s_soft[x], 1)

                        def decay(q):
                            x = q % 2
                            wait_apart(s, (s_dt[x], 2 * j + q // 2 + 1))
                            for i, d in enumerate((dec0, dec1)):
                                last = s.activation(d[x], soft[x], ACT.Exp,
                                                    scale=rate[:, bass.ds(j, 1), i:i + 1].rearrange("p k t -> p (k t)"))
                            last.then_inc(s_decay[x], 1)

                        softplus(0)
                        for q in range(1, NQ):
                            softplus(q)
                            decay(q - 1)
                        decay(NQ - 1)
                        ck.end(2 * NQ)

                @block.vector
                def _(v):
                    VCK = 8 * NQ
                    with v.Fori(0, KC) as j:
                        ck = Chain(v, s_vch, VCK * j)

                        def edges(e):
                            edges_vector(v, quads + j * QUADS_P2 + e // QC, e % QC, raw, j * QUADS_P2 + e // QC)

                        for q in range(NQ):
                            x = q % 2
                            cols = slice(q * QW, (q + 1) * QW)
                            u = act[:, bass.ds(j, 1), cols].rearrange("p k n -> p (k n)")
                            bm0, bm1, cm0, cm1 = (big[:, i, cols] for i in range(4))
                            v.wait_ge(s_soft[x], 2 * j + q // 2 + 1)
                            v.tensor_tensor(soft[x], soft[x], relu[x], ALU.add).then_inc(s_dt[x], 1)
                            edges(3 * q)
                            v.wait_ge(s_dt[x], 2 * j + q // 2 + 1)
                            ck(v.tensor_tensor(dtu[x], soft[x], u, ALU.mult))
                            v.tensor_tensor(h0[x], dtu[x], bm0, ALU.mult)
                            ck(v.tensor_tensor(h1[x], dtu[x], bm1, ALU.mult))
                            v.wait_ge(s_decay[x], 2 * j + q // 2 + 1)
                            for d in (dec0, dec1):
                                op = v.memset(d[x].rearrange("p (b n) -> p b n", n=P)[:, :, 0:1], 0.0)
                            ck(op)
                            v.tensor_tensor_scan(h0[x], dec0[x], h0[x], 0.0, ALU.mult, ALU.add)
                            scanned = ck.mark(v.tensor_tensor_scan(h1[x], dec1[x], h1[x], 0.0, ALU.mult, ALU.add))
                            edges(3 * q + 1)
                            ck.wait(scanned)
                            v.tensor_tensor(h0[x], h0[x], cm0, ALU.mult)
                            ck(v.tensor_tensor(h1[x], h1[x], cm1, ALU.mult))
                            ck(v.tensor_tensor(h0[x], h0[x], h1[x], ALU.add))
                            ck(v.scalar_tensor_tensor(out=h0[x], in0=u, scalar=skip[:, bass.ds(j, 1)], in1=h0[x],
                                                      op0=ALU.mult, op1=ALU.add))
                            v.wait_ge(s_gz[x], 32 * j + 16 * (q // 2) + 16)
                            ck(v.tensor_tensor(u, h0[x], gz[x], ALU.mult))
                            v.sem_inc(s_y[x], 1)
                            edges(3 * q + 2)
                        ck.end(8 * NQ)

                @block.gpsimd
                def _(g):
                    edges_gpsimd(g, quads, KC * QUADS_P2)
            quads += KC * QUADS_P2

            s_wo = sem_l("s_wo" + n)
            s_gb = sem_l("s_gb" + n)
            s_oa = sem_l("s_oa" + n)
            s_op = sem_l("s_op" + n)
            s_ov = sem_l("s_ov" + n)
            s_ox = sem_l("s_ox" + n)
            with ExitStack() as st, nc.Block() as block:
                raw = edges_buffer("out" + n, B, st)
                if m == 2:
                    raw = (raw[0], raw[1] + 1)
                ys = sb("ys" + n, [P, KC, P], F32, st)
                sn = sb("sn" + n, [P, S], F32, st)
                ln_g = sb("ln_g" + n, [P, S], F32, st)
                ln_b = sb("ln_b" + n, [P, S], F32, st)
                stats = sb("stats" + n, [P, HALF, 6], F32, st)
                mv = sb("mv" + n, [P, 2], F32, st)
                dev = sb("dev" + n, [P, 1], F32, st)
                rstd = sb("rstd" + n, [P, 1], F32, st)
                w_mid = sb("w_mid" + n, [P, P], F32, st)
                rb = sb("rb" + n, [P, S], F32, st)
                xb = sb("xb" + n, [P, S], F32, st)
                w_out = big[:].rearrange("p k n -> p (k n)").rearrange("p (k n) -> p k n", k=KC)
                po, pt = conv_ps[:, 0:2, :], conv_ps[:, 2:4, :]
                NA, NP, NV = 3, 2 if m == 1 else 1, 8 if m == 1 else 10

                @block.sync
                def _(sp):
                    if m == 1:
                        edges_load(sp, raw[0], quads + 1, B)
                    else:
                        edges_load(sp, raw[0], quads + 1, B - 1)
                        edges_load(sp, raw[0][:, :, B - 1:B, :], quads, 1)
                    sp.dma_start(w_out, w["WoutT"].rearrange("(k p) n -> p k n", p=P)).then_inc(s_wo, 16)
                    sp.dma_start(ln_g[:], a[f"ln{m}_g"].rearrange("(o n) -> o n", o=1).partition_broadcast(P)
                                 .rearrange("p o n -> p (o n)")).then_inc(s_gb, 16)
                    sp.dma_start(ln_b[:], a[f"ln{m}_b"].rearrange("(o n) -> o n", o=1).partition_broadcast(P)
                                 .rearrange("p o n -> p (o n)")).then_inc(s_gb, 16)
                    if m == 1:
                        sp.dma_start(w_mid[:], a["w_midT"]).then_inc(s_wo, 16)
                    else:
                        with sp.Fori(0, B) as b:
                            sp.wait_ge(s_ov, NV * b)
                            sp.dma_start(rb[:], r_d[bass.ds(b, 1)].rearrange("o c s -> (o c) s")).then_inc(s_ox, 16)
                            sp.dma_start(xb[:], x_in[bass.ds(b, 1)].rearrange("o c s -> (o c) s")).then_inc(s_ox, 16)

                @block.scalar
                def _(s):
                    with s.Fori(0, B) as b:
                        wait_apart(s, (s_op, NP * b))
                        s.activation(ys[:], act[:, :, bass.ds(b * P, P)], ACT.Copy).then_inc(s_oa, 1)
                        s.wait_ge(s_ov, NV * b + 3)
                        s.activation(dev[:], mv[:, 1:2], ACT.Sqrt, bias=eps5[:, 0:1]).then_inc(s_oa, 1)
                        if m == 1:
                            wait_apart(s, (s_op, NP * b + 2))
                            s.activation(xT[:, :, bass.ds(b * P, P)],
                                         pt.rearrange("p h n -> p (h n)").rearrange("p (k n) -> p k n", k=KC),
                                         ACT.Silu).then_inc(s_oa, 1)
                        else:
                            s.wait_ge(s_ov, NV * b + 8)
                            s.activation(rb[:], rb[:], ACT.Silu).then_inc(s_oa, 1)

                @block.tensor
                def _(t):
                    t.wait_ge(s_wo, 32 if m == 1 else 16)
                    with t.Fori(0, B) as b:
                        t.wait_ge(s_oa, NA * b + 1)
                        t.wait_ge(s_ov, NV * b)
                        for h in range(HALF):
                            for k in range(KC):
                                last = t.matmul(po[:, h], ys[:, k, :], w_out[:, k, h * QW:(h + 1) * QW],
                                                start=(k == 0), stop=(k == KC - 1))
                            if h:
                                last.then_inc(s_op, 1)
                            edges_tensor(t, quads + b, h)
                        edges_tensor(t, quads + b, 2)
                        if m == 1:
                            t.wait_ge(s_ov, NV * b + NV)
                            t.wait_ge(s_oa, NA * b)
                            for k in range(KC):
                                last = t.matmul(pt[:, k // 4, (k % 4) * P:(k % 4 + 1) * P], sn[:, k * P:(k + 1) * P],
                                                w_mid[:], start=True, stop=True)
                            last.then_inc(s_op, 1)
                        edges_tensor(t, quads + b, 3)

                @block.vector
                def _(v):
                    v.wait_ge(s_gb, 32)
                    with v.Fori(0, B) as b:
                        ck = Chain(v, s_ov, NV * b)
                        edges_vector(v, quads + b, 0)
                        edges_vector(v, quads + b, 1)
                        v.wait_ge(s_op, NP * b + 1)
                        for h in range(HALF):
                            ck(v.bn_stats(stats[:, h, :], po[:, h]), wait_apart)
                        ck(v.bn_aggr(mv[:], stats[:].rearrange("p h n -> p (h n)")))
                        v.wait_ge(s_oa, NA * b + 2)
                        ck(v.reciprocal(rstd[:], dev[:]))
                        if m == 1:
                            v.wait_ge(s_op, NP * b)
                        ck(v.tensor_scalar(sn[:], po.rearrange("p h n -> p (h n)"), mv[:, 0:1], rstd[:, 0:1],
                                           ALU.subtract, ALU.mult))
                        ck(v.tensor_tensor(sn[:], sn[:], ln_g[:], ALU.mult))
                        ck(v.tensor_tensor(sn[:], sn[:], ln_b[:], ALU.add))
                        if m == 1:
                            v.sem_inc(s_ov, 1)
                        else:
                            v.wait_ge(s_ox, 32 * b + 32)
                            ck(v.tensor_tensor(rb[:], sn[:], rb[:], ALU.add))
                            v.wait_ge(s_oa, NA * b + 3)
                            ck(v.tensor_tensor(x2[:, bass.ds(b * S, S)], rb[:], xb[:], ALU.add))
                            v.sem_inc(s_ov, 1)
                        edges_vector(v, quads + b, 2)
                        edges_vector(v, quads + b, 3, raw, b)

                @block.gpsimd
                def _(g):
                    edges_gpsimd(g, quads, B * QUADS_OUT)
            quads += B * QUADS_OUT
            lstack.close()
            nc.clear_and_free_semaphores(layer_sems)
            nc.all_engine_barrier()
        assert quads == QUADS, quads
        if stop == 1:
            with nc.Block() as block:
                @block.sync
                def _(sp):
                    sp.dma_start(a["dbg_x2"], xT[:].rearrange("p k n -> p (k n)")).then_inc(s_dst, 16)
                    sp.wait_ge(s_dst, 32)
            return

        mstack.close()
        estack.close()

        a_dst = sb("a_dst", [P, BINS, HEADS], F32)
        peak = sb("peak", [P, BINS, HEADS], F32)
        total = sb("total", [P, BINS, HEADS, EXP + 1], F32)
        bins_sb = sb("bins_sb", [1, CHUNKS + 1], I32)
        H16 = HEADS * EXP
        SPLIT = 2 * (H16 + HEADS)
        NSP = 3 * HEADS

        s_tw = sem("s_tw")
        s_tz = sem("s_tz")
        s_tv = sem("s_tv")
        s_ta = sem("s_ta")
        s_tp = sem("s_tp")
        s_tab = sem("s_tab")
        with ExitStack() as st, nc.Block() as block:
            stat_ps = ps("stat_ps", [P, 2, HALF, QW], F32, st)
            h_ps = ps("h_ps", [P, KC, H16], F32, st)
            tn = sb("tn", [P, S], F32, st)
            dv = sb("dv", [P, S], F32, st)
            rows = sb("rows", [P, KC, ROW], F32, st)
            rows_b = rows[:].rearrange("p t f -> p (t f)").bitcast(BF16).rearrange("p (t f) -> p t f", f=2 * ROW)
            weighed = sb("weighed", [P, KC, HEADS, EXP], F32, st)
            weighed2 = sb("weighed2", [P, KC, HEADS, EXP], F32, st)
            rest = sb("rest", [P, KC, HEADS], F32, st)
            logit = sb("logit", [P, KC, HEADS], F32, st)
            w_gat = sb("w_gat", [P, H16], F32, st)
            att_s = sb("att_s", [P, H16], F32, st)
            att_d = sb("att_d", [P, H16], F32, st)
            zrow = sb("zrow", [1, ROW], F32, st)
            mean_ps, var_ps = (stat_ps[:, i].rearrange("p h n -> p (h n)") for i in range(2))
            NV, NA, NP = 15, 3, 3
            full = [P, KC, HEADS, EXP]

            @block.sync
            def _(sp):
                for n in range(QC):
                    sp.wait_ge(s_scat[n], 16 * CH * QUADS)
                sp.dma_start(w_gat[:], a["W_gat"]).then_inc(s_tw, 16)
                for to, name in ((att_s, "att_src"), (att_d, "att_dst")):
                    sp.dma_start(to[:], a[name].rearrange("(o h) e -> o (h e)", o=1).partition_broadcast(P)
                                 .rearrange("p o n -> p (o n)")).then_inc(s_tw, 16)
                sp.dma_start(bins_sb[:], scr["bins"]).then_inc(s_tw, 16)
                sp.wait_ge(s_tz, 2)
                sp.dma_start(tab_d[M:M + 1, :], zrow[:]).then_inc(s_tab, 16)
                with sp.Fori(0, B) as b:
                    sp.wait_ge(s_tv, NV * b + 13)
                    sp.dma_start(tab_d[bass.ds(b * S, S), :].rearrange("(t p) f -> p t f", p=P),
                                 rows[:]).then_inc(s_tab, 16)
                sp.wait_ge(s_tab, 16 * B + 16)

            @block.vector
            def _(v):
                v.memset(rows[:], 0.0).then_inc(s_tz, 1)
                v.memset(zrow[:], 0.0).then_inc(s_tz, 1)
                v.wait_ge(s_tz, 2)
                v.wait_ge(s_tw, 64)
                with v.Fori(0, B) as b:
                    ck = Chain(v, s_tv, NV * b)
                    tiles = bass.ds(b * KC, KC)
                    v.wait_ge(s_tp, NP * b + 1)
                    v.wait_ge(s_ta, NA * b)
                    ck(v.tensor_tensor(tn[:], x2[:, bass.ds(b * S, S)], mean_ps, ALU.subtract))
                    v.wait_ge(s_ta, NA * b + 2)
                    ck(v.reciprocal(dv[:], dv[:]))
                    ck(v.tensor_tensor(tn[:], tn[:], dv[:], ALU.mult))
                    v.wait_ge(s_tp, NP * b + 3)
                    v.wait_ge(s_tab, 16 * b + 16)
                    h_view = rows[:, :, 0:H16].rearrange("p t (h e) -> p t h e", e=EXP)
                    src_log = rows[:, :, H16:H16 + HEADS]
                    ck(v.tensor_copy(rows[:, :, 0:H16], h_ps[:]))
                    for att, prod_ in ((att_s, weighed), (att_d, weighed2)):
                        op = v.tensor_tensor(prod_[:], h_view, att[:].rearrange("p (h e) -> p h e", e=EXP)
                                             .unsqueeze(1).to_broadcast(full), ALU.mult)
                    ck(op)
                    v.tensor_reduce(src_log, weighed[:], AX.X, ALU.add)
                    ck(v.tensor_reduce(a_dst[:, tiles, :], weighed2[:], AX.X, ALU.add))
                    part = [rows_b[:, :, SPLIT + HEADS * i:SPLIT + HEADS * (i + 1)] for i in range(3)]
                    ck(v.tensor_copy(part[0], src_log))
                    ck(v.tensor_tensor(rest[:], src_log, part[0], ALU.subtract))
                    ck(v.tensor_copy(part[1], rest[:]))
                    ck(v.tensor_tensor(rest[:], rest[:], part[1], ALU.subtract))
                    ck(v.tensor_copy(part[2], rest[:]))
                    ck(v.tensor_tensor(logit[:], src_log, a_dst[:, tiles, :], ALU.add), wait_apart)
                    v.tensor_copy(total[:, tiles, :, 0:EXP], h_view)
                    ck(v.tensor_copy(total[:, tiles, :, EXP], ones[:, 0:KC * HEADS].rearrange("p (t h) -> p t h", t=KC)))
                    ck(v.scalar_tensor_tensor(out=peak[:, tiles, :], in0=logit[:], scalar=0.2, in1=logit[:],
                                              op0=ALU.mult, op1=ALU.max))
                    v.sem_inc(s_tv, 1)
                    ck.end(NV - 1)

            @block.scalar
            def _(s):
                with s.Fori(0, B) as b:
                    s.wait_ge(s_tv, NV * b + 1)
                    s.activation(dv[:], tn[:], ACT.Square).then_inc(s_ta, 1)
                    s.wait_ge(s_tp, NP * b + 2)
                    s.wait_ge(s_ta, NA * b + 1)
                    s.activation(dv[:], var_ps, ACT.Sqrt, bias=eps5[:, 0:1]).then_inc(s_ta, 1)
                    wait_apart(s, (s_tv, NV * b + 3))
                    s.activation(tokens[:, bass.ds(b * S, S)], tn[:], ACT.Copy).then_inc(s_ta, 1)

            @block.tensor
            def _(t):
                t.wait_ge(s_tw, 64)
                with t.Fori(0, B) as b:
                    t.wait_ge(s_tv, NV * b)
                    for h in range(HALF):
                        last = t.matmul(stat_ps[:, 0, h], inv_c[:], x2[:, bass.ds(b * S + h * QW, QW)],
                                        start=True, stop=True)
                    last.then_inc(s_tp, 1)
                    t.wait_ge(s_ta, NA * b + 1)
                    for h in range(HALF):
                        last = t.matmul(stat_ps[:, 1, h], inv_c[:], dv[:, h * QW:(h + 1) * QW],
                                        start=True, stop=True)
                    last.then_inc(s_tp, 1)
                    t.wait_ge(s_tv, NV * b + 3)
                    for k in range(KC):
                        last = t.matmul(h_ps[:, k, :], tn[:, k * P:(k + 1) * P], w_gat[:], start=True, stop=True)
                    last.then_inc(s_tp, 1)

        SL = 4
        s_sel = sem("s_sel")
        s_pk = [sem(f"s_pk{x}") for x in range(SL)]
        s_gat = [sem(f"s_gat{x}") for x in range(SL)]
        s_src = sem("s_src")
        s_oh = sem("s_oh")
        s_otp = sem("s_otp")
        s_ot = sem("s_ot")
        s_stp = sem("s_stp")
        s_spl = sem("s_spl")
        s_bc = sem("s_bc")
        s_max = sem("s_max")
        s_resc = sem("s_resc")
        s_pg = sem("s_pg")
        s_q = sem("s_q")
        s_wgt = sem("s_wgt")
        s_msg = sem("s_msg")
        s_pa2 = sem("s_pa2")
        s_sum = sem("s_sum")
        s_gch = sem("s_gch")
        with ExitStack() as st, nc.Block() as block:
            packed = sb("packed", [P, SL, EC], I32, st)
            src_i = sb("src_i", [P, SL, EC], I32, st)
            lo_i = sb("lo_i", [P, EC], I32, st)
            lo_f = sb("lo_f", [P, EC], F32, st)
            got = sb("got", [P, SL, EC, ROW], F32, st)
            pick = sb("pick", [P, SL, EC, P], F32, st)
            pickT = sb("pickT", [P, 2, CE], F32, st)
            away = sb("away", [P, 2, CE], F32, st)
            split = sb("split", [NSP, CE], BF16, st)
            sel3 = sb("sel3", [NSP, HEADS, P], BF16, st)
            junk = sb("junk", [P, HEADS, CE], F32, st)
            cmax = sb("cmax", [P, HEADS], F32, st)
            edge_l = sb("edge_l", [P, HEADS], F32, st)
            leak = sb("leak", [P, HEADS], F32, st)
            node = sb("node", [P, 2 * HEADS], F32, st)
            fall = sb("fall", [P, HEADS], F32, st)
            resc = sb("resc", [P, 2, HEADS], F32, st)
            zl = sb("zl", [P, EC, HEADS], F32, st)
            zk = sb("zk", [P, EC, HEADS], F32, st)
            zq = sb("zq", [P, EC, HEADS], F32, st)
            msg = sb("msg", [P, 2, EC, HEADS, EXP + 1], F32, st)
            far_b = sb("far_b", [P, 1], F32, st)
            pickT_ps = ps("pickT_ps", [P, CE], F32, st)
            bc_ps = ps("bc_ps", [P, HEADS, CE], F32, st)
            split_ps = ps("split_ps", [P, 2 * QW], BF16, st)
            node_ps = ps("node_ps", [P, QW], F32, st)
            sum_ps = ps("sum_ps", [P, QW], F32, st)
            node_v = node_ps[:, 0:EC * 2 * HEADS].rearrange("p (t f) -> p t f", t=EC)
            sum_v = sum_ps[:, 0:HEADS * (EXP + 1)]

            def rounds(eng):
                return eng.value_load(bins_sb[0:1, CHUNKS:CHUNKS + 1], min_val=1, max_val=(CHUNKS - 8) // SL)

            @block.sync
            def _(sp):
                def load(i, d):
                    sp.dma_start(packed[:, d % SL, :], slots_d[bass.ds((i * SL + d) * CE, CE), :]
                                 .rearrange("(p f) o -> p (f o)", p=P)).then_inc(s_pk[d % SL], 16)

                for d in range(3):
                    load(0, d)
                with sp.Fori(0, rounds(sp)) as i:
                    for u in range(SL):
                        sp.wait_ge(s_src, SL * i + u)
                        load(i, u + 3)

            @block.gpsimd
            def _(g):
                g.memset(sel3[:], 0.0).then_inc(s_sel, 1)
                g.memset(far_b[:], -BIG).then_inc(s_sel, 1)
                for k in range(3):
                    g.wait_ge(s_sel, 2 + k)
                    g.affine_select(out=sel3[:], in_=sel3[:], compare_op=ALU.not_equal, fill=1.0, base=-HEADS * k,
                                    pattern=[[-1, HEADS], [0, P]], channel_multiplier=1).then_inc(s_sel, 1)

                def gather(i, d):
                    wait_apart(g, (s_src, SL * i + d + 1))
                    for t in range(EC):
                        g.indirect_dma_start(got[:, d % SL, t, :], None, tab_d[:, :],
                                             bass.IndirectOffsetOnAxis(ap=src_i[:, d % SL, t:t + 1], axis=0))\
                            .then_inc(s_gat[d % SL], 16)

                for d in range(2):
                    gather(0, d)
                with g.Fori(0, rounds(g)) as i:
                    for u in range(SL):
                        gather(i, u + 2)

            @block.vector
            def _(v):
                def bin_of(i, d):
                    return v.value_load(bins_sb[0:1, bass.ds(i * SL + d, 1)], min_val=0, max_val=BINS - 1)

                def unpack(i, d, ck):
                    x = d % SL
                    v.wait_ge(s_pk[x], 16 * (i + d // SL) + 16)
                    v.tensor_scalar(src_i[:, x, :], packed[:, x, :], (1 << SRC_BITS) - 1, None, ALU.bitwise_and)
                    ck(v.tensor_scalar(lo_i[:], packed[:, x, :], SRC_BITS, None, ALU.logical_shift_right))
                    v.sem_inc(s_src, 1)
                    ck(v.tensor_copy(lo_f[:], lo_i[:]))
                    for t in range(EC):
                        last = v.tensor_scalar(pick[:, x, t, :], iota_b[:], lo_f[:, t:t + 1], None, ALU.is_equal)
                    last.then_inc(s_oh, 1)
                    v.wait_ge(s_oh, SL * i + d + 1)

                def maxima(i, d, ck):
                    bin_ = bin_of(i, d)
                    wait_apart(v, (s_ot, SL * i + d + 1), (s_bc, SL * i + d + 1))
                    for h in range(HEADS):
                        op = v.tensor_tensor_reduce(junk[:, h, :], away[:, d % 2, :], bc_ps[:, h, :], 1.0, -BIG,
                                                    ALU.add, ALU.max, cmax[:, h:h + 1])
                    ck(op, wait_apart)
                    ad = a_dst[:, bass.ds(bin_, 1), :].rearrange("p b h -> p (b h)")
                    pk = peak[:, bass.ds(bin_, 1), :].rearrange("p b h -> p (b h)")
                    v.tensor_copy(node[:, 0:HEADS], ad)
                    ck(v.tensor_tensor(edge_l[:], cmax[:], ad, ALU.add))
                    ck(v.scalar_tensor_tensor(out=leak[:], in0=edge_l[:], scalar=0.2, in1=edge_l[:],
                                              op0=ALU.mult, op1=ALU.max))
                    ck(v.tensor_tensor(node[:, HEADS:], leak[:], pk, ALU.max))
                    v.wait_ge(s_resc, SL * i + d)
                    ck(v.tensor_tensor(fall[:], pk, node[:, HEADS:], ALU.subtract), wait_apart)
                    ck(v.tensor_copy(pk, node[:, HEADS:]))
                    v.sem_inc(s_max, 1)

                def logits(i, d, ck):
                    x = d % SL
                    v.wait_ge(s_pg, SL * i + d + 1)
                    ck(v.tensor_tensor(zl[:], got[:, x, :, H16:H16 + HEADS], node_v[:, :, 0:HEADS], ALU.add))
                    ck(v.scalar_tensor_tensor(out=zk[:], in0=zl[:], scalar=0.2, in1=zl[:],
                                              op0=ALU.mult, op1=ALU.max))
                    ck(v.tensor_tensor(zq[:], zk[:], node_v[:, :, HEADS:], ALU.subtract))
                    v.sem_inc(s_q, 1)

                def messages(i, d, ck):
                    x = d % SL
                    v.wait_ge(s_wgt, SL * i + d + 1)
                    ck(v.tensor_tensor(msg[:, d % 2, :, :, 0:EXP],
                                       got[:, x, :, 0:H16].rearrange("p t (h e) -> p t h e", e=EXP),
                                       msg[:, d % 2, :, :, EXP:EXP + 1].to_broadcast([P, EC, HEADS, EXP]), ALU.mult))
                    v.sem_inc(s_msg, 1)

                def sums(i, d, ck, done):
                    bin_ = bin_of(i, d)
                    v.wait_ge(s_pa2, done)
                    v.wait_ge(s_resc, done)
                    tot_ = total[:, bass.ds(bin_, 1), :, :].rearrange("p b h e -> p (b h) e")
                    ck(v.tensor_tensor(tot_, tot_, resc[:, (d + SL) % 2, :].unsqueeze(2)
                                       .to_broadcast([P, HEADS, EXP + 1]), ALU.mult))
                    ck(v.tensor_tensor(tot_, tot_, sum_v.rearrange("p (h e) -> p h e", h=HEADS), ALU.add))
                    v.sem_inc(s_sum, 1)

                v.wait_ge(s_sel, 5)
                ck = Chain(v, s_gch, 0)
                unpack(0, 0, ck)
                unpack(0, 1, ck)
                maxima(0, 0, ck)
                pre = ck.n
                per = SL * (3 + 1 + 2 + 2 + 6)
                with v.Fori(0, rounds(v)) as i:
                    ck = Chain(v, s_gch, pre + per * i)
                    for u in range(SL):
                        logits(i, u, ck)
                        unpack(i, u + 2, ck)
                        messages(i, u, ck)
                        maxima(i, u + 1, ck)
                        sums(i, u, ck, SL * i + u + 1)
                    ck.end(per)

            @block.scalar
            def _(s):
                def transposed(i, d):
                    s.wait_ge(s_otp, SL * i + d + 1)
                    if d >= 2:
                        s.wait_ge(s_pg, SL * i + d - 1)
                        s.wait_ge(s_max, SL * i + d - 1)
                    s.activation(pickT[:, d % 2, :], pickT_ps[:], ACT.Copy)
                    s.activation(away[:, d % 2, :], pickT_ps[:], ACT.Identity, bias=far_b[:, 0:1],
                                 scale=BIG).then_inc(s_ot, 1)

                def parts(i, d):
                    s.wait_ge(s_stp, SL * i + d + 1)
                    s.wait_ge(s_bc, SL * i + d)
                    s.activation(split[:], split_ps[0:NSP, 0:CE], ACT.Copy).then_inc(s_spl, 1)

                def weights(i, d):
                    s.wait_ge(s_q, SL * i + d + 1)
                    s.activation(msg[:, d % 2, :, :, EXP:EXP + 1].rearrange("p t h o -> p t (h o)"), zq[:],
                                 ACT.Exp).then_inc(s_wgt, 1)

                def rescale(i, d):
                    s.wait_ge(s_max, SL * i + d + 1)
                    s.activation(resc[:, d % 2, :], fall[:], ACT.Exp).then_inc(s_resc, 1)

                s.wait_ge(s_sel, 5)
                transposed(0, 0)
                transposed(0, 1)
                parts(0, 0)
                rescale(0, 0)
                with s.Fori(0, rounds(s)) as i:
                    for u in range(SL):
                        weights(i, u)
                        parts(i, u + 1)
                        transposed(i, u + 2)
                        rescale(i, u + 1)

            @block.tensor
            def _(t):
                def transpose_pick(i, d):
                    t.wait_ge(s_oh, SL * i + d + 1)
                    t.wait_ge(s_ot, SL * i + d)
                    for k in range(EC):
                        last = t.transpose(pickT_ps[:, k * P:(k + 1) * P], pick[:, d % SL, k, :], ident[:])
                    last.then_inc(s_otp, 1)

                def transpose_parts(i, d):
                    t.wait_ge(s_gat[d % SL], 16 * EC * (i + d // SL) + 16 * EC)
                    t.wait_ge(s_spl, SL * i + d)
                    for k in range(EC):
                        parts_ = got[:, d % SL, k, SPLIT // 2:SPLIT // 2 + NSP // 2].bitcast(BF16)
                        last = t.transpose(split_ps[0:NSP, k * P:(k + 1) * P], parts_, ident_b[:])
                    last.then_inc(s_stp, 1)

                def broadcast(i, d):
                    t.wait_ge(s_spl, SL * i + d + 1)
                    t.wait_ge(s_max, SL * i + d)
                    for h in range(HEADS):
                        last = t.matmul(bc_ps[:, h, :], sel3[:, h, :], split[:], start=True, stop=True)
                    last.then_inc(s_bc, 1)

                def node_values(i, d):
                    t.wait_ge(s_max, SL * i + d + 1)
                    t.wait_ge(s_q, SL * i + d)
                    t.wait_ge(s_ot, SL * i + d + 1)
                    for k in range(EC):
                        last = t.matmul(node_v[:, k, :], pickT[:, d % 2, k * P:(k + 1) * P], node[:],
                                        start=True, stop=True)
                    last.then_inc(s_pg, 1)

                def scatter(i, d):
                    t.wait_ge(s_msg, SL * i + d + 1)
                    t.wait_ge(s_sum, SL * i + d)
                    for k in range(EC):
                        last = t.matmul(sum_v, pick[:, d % SL, k, :],
                                        msg[:, d % 2, k].rearrange("p h e -> p (h e)"),
                                        start=(k == 0), stop=(k == EC - 1))
                    last.then_inc(s_pa2, 1)

                t.wait_ge(s_sel, 5)
                transpose_pick(0, 0)
                transpose_pick(0, 1)
                transpose_parts(0, 0)
                broadcast(0, 0)
                node_values(0, 0)
                with t.Fori(0, rounds(t)) as i:
                    for u in range(SL):
                        transpose_parts(i, u + 1)
                        broadcast(i, u + 1)
                        transpose_pick(i, u + 2)
                        scatter(i, u)
                        node_values(i, u + 1)

        gates = sb("gates", [P, BINS, EXP], F32)
        s_nw = sem("s_nw")
        s_nch = sem("s_nch")
        s_nv = sem("s_nv")
        s_na = sem("s_na")
        with ExitStack() as st, nc.Block() as block:
            agg = sb("agg", [P, BINS, HEADS, EXP], F32, st)
            agg2 = sb("agg2", [P, BINS, H16], F32, st)
            rec = sb("rec", [P, BINS, HEADS], F32, st)
            vec = [sb(f"vec{i}", [P, BINS], F32, st) for i in range(3)]
            rank = sb("rank", [P, BINS, EXP], F32, st)
            beats = sb("beats", [P, BINS], F32, st)
            score = sb("score", [P, BINS, EXP], F32, st)
            e_score = sb("e_score", [P, BINS, EXP], F32, st)
            params = sb("params", [P, 3, H16], F32, st)
            agg_f = agg[:].rearrange("p n h e -> p n (h e)")
            wide = [P, BINS, H16]

            @block.sync
            def _(sp):
                for i, name in enumerate(("b_gat", "ln_gamma", "ln_beta")):
                    sp.dma_start(params[:, i, :], a[name].rearrange("(o n) -> o n", o=1).partition_broadcast(P)
                                 .rearrange("p o n -> p (o n)")).then_inc(s_nw, 16)

            @block.scalar
            def _(s):
                s.wait_ge(s_nv, 1)
                s.activation(vec[1][:], vec[0][:], ACT.Sqrt, bias=eps5[:, 0:1], scale=1.0 / H16).then_inc(s_na, 1)
                s.wait_ge(s_nv, 2)
                s.activation(e_score[:], rank[:], ACT.Exp).then_inc(s_na, 1)

            @block.vector
            def _(v):
                ck = Chain(v, s_nch)

                def spread(x, n):
                    return x.unsqueeze(2).to_broadcast([P, BINS, n])

                def param(i):
                    return params[:, i, :].unsqueeze(1).to_broadcast(wide)

                ck(v.tensor_scalar(rec[:], total[:, :, :, EXP:EXP + 1].rearrange("p n h o -> p n (h o)"), 1e-16, None,
                                   ALU.add))
                ck(v.reciprocal(rec[:], rec[:]))
                for h in range(HEADS):
                    op = v.tensor_tensor(agg[:, :, h, :], total[:, :, h, 0:EXP], spread(rec[:, :, h], EXP), ALU.mult)
                ck(op)
                v.wait_ge(s_nw, 48)
                ck(v.tensor_tensor(agg_f, agg_f, param(0), ALU.add))
                ck(v.tensor_reduce(vec[0][:], agg_f, AX.X, ALU.add))
                ck(v.tensor_scalar(vec[0][:], vec[0][:], 1.0 / H16, None, ALU.mult))
                ck(v.tensor_tensor(agg_f, agg_f, spread(vec[0][:], H16), ALU.subtract))
                ck(v.tensor_tensor(agg2[:], agg_f, agg_f, ALU.mult))
                ck(v.tensor_reduce(vec[0][:], agg2[:], AX.X, ALU.add))
                v.sem_inc(s_nv, 1)
                v.wait_ge(s_na, 1)
                ck(v.reciprocal(vec[2][:], vec[1][:]))
                ck(v.tensor_tensor(agg_f, agg_f, spread(vec[2][:], H16), ALU.mult))
                ck(v.tensor_tensor(agg_f, agg_f, param(1), ALU.mult))
                ck(v.tensor_tensor(agg_f, agg_f, param(2), ALU.add))
                ck(v.tensor_reduce(score[:], agg[:].rearrange("p n h e -> p n e h"), AX.X, ALU.add))
                ck(v.tensor_scalar(score[:], score[:], 1.0 / HEADS, None, ALU.mult))
                ck(v.memset(rank[:], 0.0))
                for i in range(EXP):
                    for j in range(EXP):
                        if i != j:
                            ck(v.tensor_tensor(beats[:], score[:, :, j], score[:, :, i],
                                               ALU.is_ge if j < i else ALU.is_gt))
                            ck(v.tensor_tensor(rank[:, :, i], rank[:, :, i], beats[:], ALU.add))
                ck(v.tensor_scalar(gates[:], rank[:], 2.0, None, ALU.is_lt))
                ck(v.tensor_reduce(vec[0][:], score[:], AX.X, ALU.max))
                ck(v.tensor_tensor(rank[:], score[:], spread(vec[0][:], EXP), ALU.subtract))
                v.sem_inc(s_nv, 1)
                v.wait_ge(s_na, 2)
                ck(v.tensor_tensor(gates[:], gates[:], e_score[:], ALU.mult))
                ck(v.tensor_reduce(vec[0][:], gates[:], AX.X, ALU.add))
                ck(v.reciprocal(vec[1][:], vec[0][:]))
                ck(v.tensor_tensor(gates[:], gates[:], spread(vec[1][:], EXP), ALU.mult))

        s_mw = sem("s_mw")
        s_g4 = sem("s_g4")
        s_gtp = sem("s_gtp")
        s_gt = sem("s_gt")
        s_gb2 = sem("s_gb2")
        s_hid = sem("s_hid")
        s_gelu = sem("s_gelu")
        s_hg = sem("s_hg")
        s_used = sem("s_used")
        s_po = sem("s_po")
        s_fin = sem("s_fin")
        s_out = [sem("s_out0"), sem("s_out1")]
        with ExitStack() as st, nc.Block() as block:
            w1 = sb("w1", [P, EXP, D2], F32, st)
            w2 = sb("w2", [P, EXP, FH, P], F32, st)
            b1 = sb("b1", [P, EXP, FH], F32, st)
            b2 = sb("b2", [EXP, P], F32, st)
            g4 = sb("g4", [P, 4, EXP], F32, st)
            gT = sb("gT", [EXP, QW], F32, st)
            hid = sb("hid", [P, 2, QW], F32, st)
            hg = sb("hg", [P, 2, QW], F32, st)
            ost = sb("ost", [P, 2, QW], F32, st)
            hid_ps = ps("hid_ps", [P, 2, QW], F32, st)
            gate_ps = ps("gate_ps", [P, 2, QW], F32, st)
            out_ps = ps("out_ps", [P, QW], F32, st)
            gT_ps = ps("gT_ps", [P, QW], F32, st)
            U = EXP * FH
            out = a["out"].rearrange("b c h w -> b c (h w)")

            @block.sync
            def _(sp):
                sp.dma_start(w1[:], a["W1"].rearrange("e d f -> d e f")).then_inc(s_mw, 16)
                sp.dma_start(w2[:], a["W2"].rearrange("e (f p) d -> p e f d", p=P)).then_inc(s_mw, 16)
                with nc.allow_non_contiguous_dma(reason="small parameters, one to a partition"):
                    sp.dma_start(b1[:], a["b1"].rearrange("e (f p) -> p e f", p=P)).then_inc(s_mw, 16)
                sp.dma_start(b2[:], a["b2"]).then_inc(s_mw, 16)
                with sp.Fori(0, B) as b:
                    for h in range(HALF):
                        sp.wait_ge(s_fin, 2 * b + h + 1)
                        sp.dma_start(out[bass.ds(b, 1), :, h * QW:(h + 1) * QW].rearrange("o c s -> (o c) s"),
                                     ost[:, h, :]).then_inc(s_out[h], 16)
                for h in range(HALF):
                    sp.wait_ge(s_out[h], 16 * B)

            @block.scalar
            def _(s):
                s.wait_ge(s_mw, 64)
                with s.Fori(0, B) as b:
                    for h in range(HALF):
                        g = 2 * b + h
                        wait_apart(s, (s_gtp, g))
                        s.activation(g4[:], gates[:, bass.ds(g * 4, 4), :], ACT.Copy).then_inc(s_g4, 1)
                        s.wait_ge(s_gtp, g + 1)
                        s.wait_ge(s_used, U * g)
                        s.activation(gT[:], gT_ps[0:EXP, :], ACT.Copy).then_inc(s_gt, 1)
                        for u in range(U):
                            s.wait_ge(s_hid, U * g + u + 1)
                            if u >= 2:
                                s.wait_ge(s_hg, U * g + u - 1)
                            else:
                                s.wait_ge(s_hg, U * g)
                            s.activation(hid[:, u % 2, :], hid_ps[:, u % 2, :], ACT.Gelu,
                                         bias=b1[:, u // FH, u % FH:u % FH + 1]).then_inc(s_gelu, 1)

            @block.vector
            def _(v):
                with v.Fori(0, B) as b:
                    for h in range(HALF):
                        g = 2 * b + h
                        for u in range(U):
                            v.wait_ge(s_gelu, U * g + u + 1)
                            v.wait_ge(s_gb2, EXP * g + u // FH + 1)
                            if u >= 2:
                                v.wait_ge(s_used, U * g + u - 1)
                            else:
                                v.wait_ge(s_used, U * g)
                            v.tensor_tensor(hg[:, u % 2, :], hid[:, u % 2, :], gate_ps[:, (u // FH) % 2, :],
                                            ALU.mult).then_inc(s_hg, 1)
                        v.wait_ge(s_po, g + 1)
                        v.wait_ge(s_out[h], 16 * b)
                        v.tensor_tensor(ost[:, h, :], out_ps[:], x2[:, bass.ds(g * QW, QW)],
                                        ALU.add).then_inc(s_fin, 1)

            @block.tensor
            def _(t):
                t.wait_ge(s_mw, 64)
                with t.Fori(0, B) as b:
                    for h in range(HALF):
                        g = 2 * b + h

                        def hidden(u):
                            t.wait_ge(s_gelu, U * g + u - 1 if u >= 2 else U * g)
                            t.matmul(hid_ps[:, u % 2, :], w1[:, u // FH, (u % FH) * P:(u % FH + 1) * P],
                                     tokens[:, bass.ds(g * QW, QW)], start=True, stop=True).then_inc(s_hid, 1)

                        def gate(e):
                            t.wait_ge(s_hg, U * g + FH * (e - 1) if e >= 2 else U * g)
                            t.matmul(gate_ps[:, e % 2, :], ident[0:EXP, e:e + 1].to_broadcast([EXP, P]), gT[:],
                                     start=True, stop=True).then_inc(s_gb2, 1)

                        def project(u):
                            t.wait_ge(s_hg, U * g + u + 1)
                            op = t.matmul(out_ps[:], w2[:, u // FH, u % FH, :], hg[:, u % 2, :],
                                          start=False, stop=(u == U - 1))
                            op.then_inc(s_used, 1)

                        t.wait_ge(s_g4, g + 1)
                        t.wait_ge(s_gt, g)
                        for k in range(4):
                            last = t.transpose(gT_ps[0:EXP, k * P:(k + 1) * P], g4[:, k, :], ident[:])
                        last.then_inc(s_gtp, 1)
                        hidden(0)
                        t.wait_ge(s_gt, g + 1)
                        gate(0)
                        t.wait_ge(s_fin, g)
                        t.matmul(out_ps[:], b2[:], gT[:], start=True, stop=False)
                        for u in range(U):
                            if u + 1 < U:
                                hidden(u + 1)
                            if u % FH == 0 and u // FH + 1 < EXP:
                                gate(u // FH + 1)
                            project(u)
                        t.wait_ge(s_used, U * g + U)
                        t.sem_inc(s_po, 1)




SCRATCH = (("slots", (SLOTS, 1), I32), ("counts", (CH, P), F32), ("bins", (1, CHUNKS + 1), I32),
           ("r", (B, C, S), F32), ("sz", (KC, P, NT), F32), ("tab", (M + 1, ROW), F32))


def layouts(inputs):
    import numpy as np

    def t(name):
        return np.ascontiguousarray(np.asarray(inputs[name]).T)

    c, f = "L0_conv_", "L0_ffn_"
    got = {"x": inputs["x"], "edges": inputs[f + "edge_index"]}
    for m in ("m1_", "m2_"):
        for k in ("Win", "Wx", "Wdt", "Wout"):
            got[m + k + "T"] = t(c + m + k)
        for k in ("convw", "convb", "bdt", "Alog", "D"):
            got[m + k] = inputs[c + m + k]
    for k in ("ln1_g", "ln1_b", "ln2_g", "ln2_b", "b_spa"):
        got[k] = inputs[c + k]
    for k in ("W_mid", "W_spa", "W_res"):
        got[k.lower() + "T"] = t(c + k)
    for k in ("W_gat", "att_src", "att_dst", "b_gat", "ln_gamma", "ln_beta", "W1", "b1", "W2", "b2"):
        got[k] = inputs[f + k]
    return {k: np.ascontiguousarray(v) for k, v in got.items()}


def kernel(**inputs):
    from concourse import bacc
    from concourse.bass_utils import run_bass_kernel_spmd

    nc = bacc.Bacc("TRN2", target_bir_lowering=False, num_devices=1)
    arrays, aps = {}, {}
    for name, array in layouts(inputs).items():
        arrays["in_" + name] = array
        aps[name] = nc.dram_tensor("in_" + name, array.shape, mybir.dt.from_np(array.dtype), kind="ExternalInput").ap()
    aps["scratch"] = {name: nc.dram_tensor("scratch_" + name, shape, dt, kind="Internal").ap()
                      for name, shape, dt in SCRATCH}
    aps["out"] = nc.dram_tensor("out", (B, C, 32, 32), F32, kind="ExternalOutput").ap()
    program(nc, aps)
    return run_bass_kernel_spmd(nc, [arrays], core_ids=[0]).results[0]["out"]
```

```python
from contextlib import ExitStack

import concourse.bass as bass
from concourse import mybir

ALU = mybir.AluOpType
ACT = mybir.ActivationFunctionType
AX = mybir.AxisListType
F32 = mybir.dt.float32
BF16 = mybir.dt.bfloat16
I32 = mybir.dt.int32

P = 128
B, C, S = 16, 128, 1024
NT = B * C
KC = S // P
DTR, NST, DCONV = 64, 2, 4
XD = DTR + 2 * NST
QW = 512
NQ = NT // QW
HALF = S // QW

M = B * S
NE = 524288
BINS = M // P
HEADS, EXP = 4, 4
CH = 8
QC = 4
QF = CH * QC
QUADS = NE // (P * QF)
EC = 4
CE = EC * P
CHUNKS = NE // CE + BINS + 8
SLOTS = CHUNKS * CE
SRC_BITS = 15
NO_NODE = M
EMPTY = (P << SRC_BITS) | NO_NODE
FAR = float(1 << 20)
BIG = 1e30
ROW = 32
FH = 2
D2 = 256

SL_LOG = 3
SL = 1 << SL_LOG
QUADS_P1 = 2
QUADS_P2 = 2
QUADS_PRE = 2
QUADS_OUT = 1


class Chain:

    def __init__(self, eng, sem, base=0):
        self.eng, self.sem, self.base, self.n = eng, sem, base, 0

    def mark(self, ins):
        self.n += 1
        ins.then_inc(self.sem, 1)
        return self.n

    def wait(self, mark):
        self.eng.wait_ge(self.sem, self.base + mark)

    def __call__(self, ins, wait_apart=None):
        self.n += 1
        ins.then_inc(self.sem, 1)
        if wait_apart:
            wait_apart(self.eng, (self.sem, self.base + self.n))
        else:
            self.eng.wait_ge(self.sem, self.base + self.n)

    def end(self, per):
        assert self.n == per, (self.n, per)


def program(nc, a):
    ctx = ExitStack()
    scr = a["scratch"]

    def sem(name):
        return ctx.enter_context(nc.semaphore(name))

    with ctx:
        def sb(name, shape, dt, where=None):
            return (where or ctx).enter_context(nc.sbuf_tensor(name, shape, dt))

        def ps(name, shape, dt, where=None):
            return (where or ctx).enter_context(nc.psum_tensor(name, shape, dt))

        slots_d, counts_d, r_d, sz_d, tab_d = (scr[k] for k in ("slots", "counts", "r", "sz", "tab"))

        s_passed = sem("s_passed")

        def wait_apart(eng, *waits):
            for sem_, n in waits:
                eng.wait_ge(sem_, n)
            eng.sem_inc(s_passed, 1)

        ident = sb("ident", [P, P], F32)
        ident_b = sb("ident_b", [P, P], BF16)
        iota_b = sb("iota_b", [P, P], BF16)
        ones = sb("ones", [P, P], F32)
        inv_c = sb("inv_c", [P, P], F32)
        eps5 = sb("eps5", [P, 1], F32)
        eps6 = sb("eps6", [P, 1], F32)

        s_const = sem("s_const")
        s_dst = sem("s_dst")
        s_split = sem("s_split")
        s_hot = [sem("s_hot0"), sem("s_hot1")]
        s_hist = [sem("s_hist0"), sem("s_hist1")]
        s_histall = sem("s_histall")
        s_fill = sem("s_fill")
        s_ck = sem("s_ck")
        s_sv = sem("s_sv")
        s_sp = sem("s_sp")
        s_cnt = sem("s_cnt")
        s_cd = sem("s_cd")

        xT = sb("xT", [P, KC, NT], F32)
        act = sb("act", [P, KC, NT], F32)
        x2 = xT[:].rearrange("p k n -> p (k n)")
        tokens = act[:].rearrange("p k n -> p (k n)")

        estack = ctx.enter_context(ExitStack())
        upper = sb("upper", [P, P], BF16, estack)
        lower = sb("lower", [P, P], BF16, estack)
        hot = sb("hot", [P, QC, CH, P], BF16, estack)
        q_bin = sb("q_bin", [P, QF], I32, estack)
        q_binf = sb("q_binf", [P, QF], F32, estack)
        q_far = sb("q_far", [P, QF], F32, estack)
        q_lo = sb("q_lo", [P, QF], I32, estack)
        q_wrap = sb("q_wrap", [P, QF], F32, estack)
        q_srcf = sb("q_srcf", [P, QF], F32, estack)
        q_src = sb("q_src", [P, QF], I32, estack)
        q_pack = sb("q_pack", [P, QF], I32, estack)
        rank_f = sb("rank_f", [P, CH], F32, estack)
        prod = sb("prod", [P, CH, P], BF16, estack)
        slot_i = sb("slot_i", [P, QC, CH], I32, estack)
        pack_i = sb("pack_i", [P, QC, CH], I32, estack)

        bstack = ctx.enter_context(ExitStack())
        base_row = sb("base_row", [1, CH * P], F32, bstack)

        with ExitStack() as st:
            chunk_bin = sb("chunk_bin", [1, CHUNKS + 1], I32, st)
            NCOL = QUADS * QF
            dst = tokens[:, 0:NCOL].bitcast(I32).rearrange("p (q f) -> p q f", f=QF)
            tmp_i = tokens[:, NCOL:2 * NCOL].bitcast(I32)
            hi_a = x2[:, 0:NCOL].bitcast(BF16)[:, 0:NCOL]
            hi_b = x2[:, NCOL:2 * NCOL].bitcast(BF16)[:, 0:NCOL]
            hot_a = sb("hot_a", [P, 2, CH, 4, QC * 8], BF16, st)
            hot_b = sb("hot_b", [P, 2, P, 16], BF16, st)
            zero_b = sb("zero_b", [P, 256], BF16, st)
            fill = sb("fill", [P, SLOTS // P // 5], I32, st)
            part_i = sb("part_i", [P, 1], I32, st)
            part8 = sb("part8", [P, 1], I32, st)
            part8f = sb("part8f", [P, 1], F32, st)
            diag = sb("diag", [P, 16, 16], F32, st)
            col16 = sb("col16", [P, 16, 16], F32, st)
            masked = sb("masked", [P, 16, 16], F32, st)
            per_ab = sb("per_ab", [P, CH, 16], F32, st)
            sel_a = sb("sel_a", [P, 8], F32, st)
            cnt8 = sb("cnt8", [8, CH, 16], F32, st)
            cnt = sb("cnt", [1, CH, P], F32, st)
            tot = sb("tot", [1, P], F32, st)
            tot_i = sb("tot_i", [1, P], I32, st)
            nch_i = sb("nch_i", [1, P], I32, st)
            nch = sb("nch", [1, P], F32, st)
            ends = sb("ends", [1, P], F32, st)
            one_row = sb("one_row", [1, P], F32, st)
            ends_c = sb("ends_c", [P, 1], F32, st)
            chunk_no = sb("chunk_no", [P, CHUNKS], F32, st)
            past = sb("past", [P, CHUNKS], F32, st)
            cb_f = sb("cb_f", [1, CHUNKS], F32, st)
            round_i = sb("round_i", [1, 2], I32, st)
            ph = ps("ph", [P, CH, QW], F32, st)
            GROUPS = QUADS // 4

            with nc.Block() as block:
                @block.sync
                def _(sp):
                    sp.dma_start(dst, a["edges"][1].rearrange("(q p f) -> p q f", p=P, f=QF)).then_inc(s_dst, 16)
                    sp.wait_ge(s_const, 1)
                    for n in range(5):
                        w = SLOTS // 5
                        sp.dma_start(slots_d[n * w:(n + 1) * w, :].rearrange("(p f) o -> p (f o)", p=P),
                                     fill[:]).then_inc(s_fill, 16)
                    sp.wait_ge(s_cnt, 1)
                    for c in range(CH):
                        sp.dma_start(counts_d[c:c + 1, :].rearrange("o (h l) -> (o h) l", h=8),
                                     cnt8[:, c, :]).then_inc(s_cd, 16)
                    sp.wait_ge(s_cd, 16 * CH)
                    sp.dma_start(cnt[:].rearrange("o c b -> o (c b)"),
                                 counts_d[:, :].rearrange("(o c) b -> o (c b)", o=1)).then_inc(s_cd, 16)
                    sp.wait_ge(s_sv, 4)
                    sp.dma_start(scr["bins"], chunk_bin[:]).then_inc(s_fill, 16)
                    sp.wait_ge(s_fill, 96)

                @block.gpsimd
                def _(g):
                    g.memset(fill[:], EMPTY).then_inc(s_const, 1)
                    g.memset(ident[:], 0.0)
                    g.memset(ones[:], 1.0)
                    g.memset(inv_c[:], 1.0 / C)
                    g.memset(eps5[:], 1e-5)
                    g.memset(eps6[:], 1e-6)
                    g.memset(zero_b[:], 0.0)
                    g.memset(one_row[:], 1.0)
                    g.memset(upper[:], 1.0)
                    g.memset(lower[:], 1.0)
                    g.memset(hot[:], 0.0)
                    g.memset(sel_a[:], 0.0).then_inc(s_const, 1)
                    g.wait_ge(s_const, 2)
                    g.affine_select(out=ident[:], in_=ident[:], compare_op=ALU.not_equal, fill=1.0, base=0,
                                    pattern=[[-1, P]], channel_multiplier=1)
                    g.affine_select(out=upper[:], in_=upper[:], compare_op=ALU.is_ge, fill=0.0, base=-1,
                                    pattern=[[1, P]], channel_multiplier=-1)
                    g.affine_select(out=lower[:], in_=lower[:], compare_op=ALU.is_ge, fill=0.0, base=0,
                                    pattern=[[-1, P]], channel_multiplier=1)
                    g.iota(iota_b[:], pattern=[[1, P]], base=0, channel_multiplier=0,
                           allow_small_or_imprecise_dtypes=True)
                    g.iota(part_i[:], pattern=[[0, 1]], base=0, channel_multiplier=1)
                    g.iota(col16[:], pattern=[[1, 16], [0, 16]], base=0, channel_multiplier=0,
                           allow_small_or_imprecise_dtypes=True)
                    g.iota(chunk_no[:], pattern=[[1, CHUNKS]], base=0, channel_multiplier=0,
                           allow_small_or_imprecise_dtypes=True)
                    g.wait_ge(s_const, 2)
                    for k in range(16):
                        last = g.affine_select(out=sel_a[:], in_=sel_a[:], compare_op=ALU.not_equal, fill=1.0,
                                               base=-8 * k, pattern=[[-1, 8]], channel_multiplier=1)
                        last.then_inc(s_const, 1)
                        g.wait_ge(s_const, 3 + k)

                @block.vector
                def _(v):
                    ck = Chain(v, s_ck)
                    v.wait_ge(s_const, 18)
                    v.tensor_copy(ident_b[:], ident[:])
                    ck(v.tensor_scalar(part8[:], part_i[:], 3, None, ALU.logical_shift_right))
                    ck(v.tensor_copy(part8f[:], part8[:]))
                    ck(v.tensor_scalar(diag[:], col16[:], part8f[:, 0:1], None, ALU.is_equal))
                    v.wait_ge(s_dst, 16)
                    flat = dst.rearrange("p q f -> p (q f)")
                    ck(v.tensor_scalar(tmp_i, flat, 11, None, ALU.logical_shift_right))
                    ck(v.tensor_copy(hi_a, tmp_i))
                    ck(v.tensor_scalar(tmp_i, flat, 7, 15, ALU.logical_shift_right, ALU.bitwise_and))
                    ck(v.tensor_copy(hi_b, tmp_i))
                    with v.Fori(0, GROUPS // 2) as g:
                        for x in range(2):
                            v.wait_ge(s_hist[x], g)
                            fa = hi_a[:, bass.ds((2 * g + x) * P, P)]
                            fb = hi_b[:, bass.ds((2 * g + x) * P, P)]
                            for q in range(4):
                                v.tensor_tensor(hot_a[:, x, :, q, :].rearrange("p c (f a) -> p c f a", a=8),
                                                fa[:, q * QF:(q + 1) * QF].rearrange("p (c f) -> p c f", f=QC)
                                                .unsqueeze(3).to_broadcast([P, CH, QC, 8]),
                                                iota_b[:, 0:8].unsqueeze(1).unsqueeze(1)
                                                .to_broadcast([P, CH, QC, 8]), ALU.is_equal)
                            v.tensor_tensor(hot_b[:, x], fb.unsqueeze(2).to_broadcast([P, P, 16]),
                                            iota_b[:, 0:16].unsqueeze(1).to_broadcast([P, P, 16]),
                                            ALU.is_equal).then_inc(s_hot[x], 1)
                    v.wait_ge(s_hist[0], GROUPS // 2)
                    v.wait_ge(s_hist[1], GROUPS // 2)
                    for c in range(CH):
                        ck(v.tensor_tensor(masked[:], ph[:, c, 0:256].rearrange("p (a b) -> p a b", a=16),
                                           diag[:], ALU.mult))
                        ck(v.tensor_reduce(per_ab[:, c, :], masked[:].rearrange("p a b -> p b a"), AX.X, ALU.add))
                    v.sem_inc(s_sv, 1)
                    v.wait_ge(s_sp, 1)
                    v.tensor_copy(cnt8[:], ph[0:8, 0, 0:P].rearrange("p (c b) -> p c b", c=CH)).then_inc(s_cnt, 1)
                    v.wait_ge(s_cd, 16 * (CH + 1))
                    ck(v.tensor_reduce(tot[:], cnt[:].rearrange("o c b -> o b c"), AX.X, ALU.add))
                    ck(v.tensor_scalar(tot_i[:], tot[:], float(CE - 1), None, ALU.add))
                    ck(v.tensor_scalar(nch_i[:], tot_i[:], 9, None, ALU.logical_shift_right))
                    ck(v.tensor_copy(nch[:], nch_i[:]))
                    ck(v.tensor_tensor_scan(ends[:], one_row[:], nch[:], 0.0, ALU.mult, ALU.add))
                    ck(v.tensor_tensor(base_row[:, 0:P], ends[:], nch[:], ALU.subtract))
                    ck(v.tensor_scalar(base_row[:, 0:P], base_row[:, 0:P], float(CE), None, ALU.mult))
                    for c in range(1, CH):
                        ck(v.tensor_tensor(base_row[:, c * P:(c + 1) * P], base_row[:, (c - 1) * P:c * P],
                                           cnt[:, c - 1, :], ALU.add))
                    ck(v.tensor_scalar(round_i[:, 0:1], ends[:, P - 1:P], float(SL - 1), float(SL), ALU.add, ALU.max))
                    ck(v.tensor_scalar(chunk_bin[:, CHUNKS:CHUNKS + 1], round_i[:, 0:1], SL_LOG, None,
                                       ALU.logical_shift_right))
                    v.sem_inc(s_sv, 1)
                    v.wait_ge(s_sp, 2)
                    ck(v.tensor_copy(ends_c[:], ph[:, 1, 0:1]))
                    ck(v.tensor_scalar(past[:], chunk_no[:], ends_c[:, 0:1], None, ALU.is_ge))
                    v.sem_inc(s_sv, 1)
                    v.wait_ge(s_sp, 3)
                    for n in range(0, CHUNKS, QW):
                        w = min(QW, CHUNKS - n)
                        ck(v.tensor_scalar(chunk_bin[:, n:n + w], ph[0:1, 2 + n // QW, 0:w], float(BINS - 1), None,
                                           ALU.min))
                    v.sem_inc(s_sv, 1)

                @block.tensor
                def _(t):
                    t.wait_ge(s_const, 18)
                    for c in range(CH):
                        t.matmul(ph[:, c, 0:256], zero_b[:, 0:P], zero_b[:], start=True, stop=True)
                    with t.Fori(0, GROUPS // 2) as g:
                        for x in range(2):
                            t.wait_ge(s_hot[x], g + 1)
                            for c in range(CH):
                                la = hot_a[:, x, c].rearrange("p q f -> p (q f)")
                                rb = hot_b[:, x].rearrange("p (q f) b -> p q (f b)", q=4)[:, :, c * 64:c * 64 + 64]
                                last = t.matmul(ph[:, c, 0:256].rearrange("p (q f) -> p q f", q=4), la, rb,
                                                start=False, stop=True, skip_group_check=True)
                            last.then_inc(s_hist[x], 1)
                    t.wait_ge(s_sv, 1)
                    t.matmul(ph[0:8, 0, 0:P], sel_a[:], per_ab[:].rearrange("p c b -> p (c b)"),
                             start=True, stop=True).then_inc(s_sp, 1)
                    t.wait_ge(s_sv, 2)
                    t.matmul(ph[:, 1, 0:1], ends[:], one_row[:, 0:1], start=True, stop=True).then_inc(s_sp, 1)
                    t.wait_ge(s_sv, 3)
                    for n in range(0, CHUNKS, QW):
                        w = min(QW, CHUNKS - n)
                        last = t.matmul(ph[0:1, 2 + n // QW, 0:w], ones[:, 0:1], past[:, n:n + w],
                                        start=True, stop=True)
                    last.then_inc(s_sp, 1)

        rank_ps = ps("rank_ps", [P, 2, 4, P], F32, estack)
        s_raw = sem("s_raw")
        s_eh = sem("s_eh")
        s_rank = [sem("s_rank0"), sem("s_rank1")]
        s_ttr = [sem("s_ttr0"), sem("s_ttr1")]
        s_slot = sem("s_slot")
        s_scat = [sem(f"s_scat{n}") for n in range(QC)]
        s_eck = sem("s_eck")
        EDGE_CK = 4

        edge_src = a["edges"][0].rearrange("(q p f) -> q p f", p=P, f=QF)
        edge_dst = a["edges"][1].rearrange("(q p f) -> q p f", p=P, f=QF)

        loads = [0]

        def edges_buffer(name, n, st):
            loads[0] += 1
            return sb("raw_" + name, [P, 2, n, QF], I32, st), loads[0]

        def edges_load(sp, raw, first, n):
            for i, edges in enumerate((edge_src, edge_dst)):
                sp.dma_start(raw[:, i, 0:n, :], edges[first:first + n].rearrange("q p f -> p q f")).then_inc(s_raw, 16)

        def edges_split(v, k, src, dst_):
            ck = Chain(v, s_eck, k * EDGE_CK)
            v.tensor_scalar(q_wrap[:], src, 0.0, float(M), ALU.is_lt, ALU.mult)
            v.tensor_scalar(q_lo[:], dst_, P - 1, SRC_BITS, ALU.bitwise_and, ALU.logical_shift_left)
            ck(v.tensor_scalar(q_bin[:], dst_, 7, None, ALU.logical_shift_right))
            v.tensor_copy(q_binf[:], q_bin[:])
            ck(v.tensor_tensor(q_srcf[:], src, q_wrap[:], ALU.add))
            v.tensor_scalar(q_far[:], q_binf[:], float(BINS), FAR, ALU.is_ge, ALU.mult)
            ck(v.tensor_scalar(q_src[:], q_srcf[:], float(M - 1), 0.0, ALU.min, ALU.max))
            ck(v.tensor_tensor(q_pack[:], q_src[:], q_lo[:], ALU.bitwise_or))
            ck.end(EDGE_CK)

        def edges_hot(v, t):
            v.tensor_tensor(hot[:, t], iota_b[:].unsqueeze(1).to_broadcast([P, CH, P]),
                            q_binf[:].rearrange("p (c t) -> p t c", t=QC)[:, t, :].unsqueeze(2)
                            .to_broadcast([P, CH, P]), ALU.is_equal).then_inc(s_eh, 1)

        def edges_vector(v, k, t, raw=None, at=None):
            v.wait_ge(s_slot, QC * k + t)
            for x in range(2):
                v.wait_ge(s_rank[x], QC * k + t + 1)
                for c in range(4):
                    last = v.tensor_tensor_reduce(prod[:, 4 * x + c], hot[:, t, 4 * x + c, :],
                                                  rank_ps[:, x, c, :], 1.0, 0.0, ALU.mult, ALU.add,
                                                  rank_f[:, 4 * x + c:4 * x + c + 1])
                last.then_inc(s_ttr[x], 1)
            if t + 1 < QC:
                edges_hot(v, t + 1)
            v.wait_ge(s_ttr[0], QC * k + t + 1)
            v.wait_ge(s_ttr[1], QC * k + t + 1)
            v.wait_ge(s_scat[t], 16 * CH * k)
            v.tensor_copy(pack_i[:, t, :], q_pack[:].rearrange("p (c t) -> p t c", t=QC)[:, t, :])
            v.tensor_tensor(slot_i[:, t, :], rank_f[:],
                            q_far[:].rearrange("p (c t) -> p t c", t=QC)[:, t, :],
                            ALU.add).then_inc(s_slot, 1)
            if t == QC - 1 and raw is not None:
                tile, load = raw
                v.wait_ge(s_raw, 32 * load)
                v.wait_ge(s_slot, QC * k + QC)
                edges_split(v, k + 1, *(tile[:, i, bass.ds(at, 1), :].rearrange("p o f -> p (o f)") for i in range(2)))
                edges_hot(v, 0)

        def edges_tensor(t_, k, t):
            t_.wait_ge(s_eh, QC * k + t + 1)
            for x in range(2):
                t_.wait_ge(s_ttr[x], QC * k + t)
                t_.matmul(rank_ps[:, x], lower[:], hot[:, (t - 1) % QC, 4 * x:4 * x + 4, :],
                          start=False, stop=True, skip_group_check=True)
                t_.matmul(rank_ps[:, x], upper[:], hot[:, t, 4 * x:4 * x + 4, :],
                          start=False, stop=True, skip_group_check=True).then_inc(s_rank[x], 1)

        def edges_gpsimd(g, first, n):
            with g.Fori(first, first + n) as k:
                for t in range(QC):
                    wait_apart(g, (s_slot, QC * k + t + 1))
                    for c in range(CH):
                        g.indirect_dma_start(slots_d[:, :], bass.IndirectOffsetOnAxis(ap=slot_i[:, t, c:c + 1], axis=0),
                                             pack_i[:, t, c:c + 1], None, bounds_check=SLOTS - 1,
                                             oob_is_err=False).then_inc(s_scat[t], 16)

        s_base = sem("s_base")
        with ExitStack() as st, nc.Block() as block:
            raw, load = edges_buffer("first", 1, st)

            @block.tensor
            def _(t):
                for x in range(2):
                    last = t.matmul(rank_ps[:, x], ones[0:1, :], base_row[:, x * QW:(x + 1) * QW],
                                    start=True, stop=True)
                last.then_inc(s_base, 1)
                t.wait_ge(s_base, 1)

            @block.sync
            def _(sp):
                edges_load(sp, raw, 0, 1)

            @block.vector
            def _(v):
                v.wait_ge(s_raw, 32)
                edges_split(v, 0, raw[:, 0, 0, :], raw[:, 1, 0, :])
                edges_hot(v, 0)
        bstack.close()

        mstack = ctx.enter_context(ExitStack())
        conv_ps = ps("conv_ps", [P, 6, QW], F32, mstack)
        big = sb("big", [P, 4, NT], F32, mstack)
        x_in = a["x"].rearrange("b c h w -> b c (h w)")

        s_px = sem("s_px")
        s_pw = sem("s_pw")
        s_pv = sem("s_pv")
        s_pa = sem("s_pa")
        s_pp = sem("s_pp")
        s_pr = sem("s_pr")
        with ExitStack() as st, nc.Block() as block:
            xin = sb("xin", [P, S], F32, st)
            xc = sb("xc", [P, S], F32, st)
            sq = sb("sq", [P, S], F32, st)
            xs = sb("xs", [P, KC, P], F32, st)
            r1 = big[:, 0, 0:S]
            r2 = sb("r2", [P, S], F32, st)
            b_spa = sb("b_spa", [1, S], F32, st)
            raw = edges_buffer("pre", B * QUADS_PRE, st)
            w_res = sb("w_res", [P, P], F32, st)
            w_spa = act[:].rearrange("p k n -> p (k n)")[:, 0:KC * S].rearrange("p (k n) -> p k n", k=KC)
            pa, pb, pc = (conv_ps[:, 2 * n:2 * n + 2, :] for n in range(3))
            NV, NA, NP = 3, 6, 5

            def flat(t):
                return t.rearrange("p h n -> p (h n)")

            def edge_steps(b, first, end):
                return [(QUADS_PRE * b + e // QC, e % QC) for e in range(first, end)]

            @block.sync
            def _(sp):
                edges_load(sp, raw[0], 1, B * QUADS_PRE)
                sp.dma_start(w_spa, a["w_spaT"].rearrange("(k p) n -> p k n", p=P)).then_inc(s_pw, 16)
                sp.dma_start(b_spa[:], a["b_spa"].rearrange("(o n) -> o n", o=1)).then_inc(s_pw, 16)
                sp.dma_start(w_res[:], a["w_resT"]).then_inc(s_pw, 16)
                with sp.Fori(0, B) as b:
                    sp.wait_ge(s_pv, NV * b)
                    sp.dma_start(xin[:], x_in[bass.ds(b, 1)].rearrange("o c s -> (o c) s")).then_inc(s_px, 16)
                    sp.wait_ge(s_pa, NA * b + 6)
                    sp.dma_start(r_d[bass.ds(b, 1)].rearrange("o c s -> (o c) s"), r2[:]).then_inc(s_pr, 16)
                sp.wait_ge(s_pr, 16 * B)

            @block.vector
            def _(v):
                with v.Fori(0, B) as b:
                    v.wait_ge(s_px, 16 * b + 16)
                    v.wait_ge(s_pp, NP * b + 1)
                    v.wait_ge(s_pa, NA * b)
                    v.tensor_tensor(xc[:], xin[:], flat(pa), ALU.subtract).then_inc(s_pv, 1)
                    for quad, e in edge_steps(b, 0, 1):
                        edges_vector(v, quad, e)
                    v.wait_ge(s_pa, NA * b + 2)
                    v.reciprocal(sq[:], sq[:]).then_inc(s_pv, 1)
                    v.wait_ge(s_pv, NV * b + 2)
                    v.tensor_tensor(xc[:], xc[:], sq[:], ALU.mult).then_inc(s_pv, 1)
                    for quad, e in edge_steps(b, 1, QUADS_PRE * QC):
                        edges_vector(v, quad, e, raw, quad)

            @block.scalar
            def _(s):
                with s.Fori(0, B) as b:
                    s.wait_ge(s_pv, NV * b + 1)
                    s.activation(sq[:], xc[:], ACT.Square).then_inc(s_pa, 1)
                    s.wait_ge(s_pp, NP * b + 2)
                    s.wait_ge(s_pa, NA * b + 1)
                    s.activation(sq[:], flat(pb), ACT.Sqrt, bias=eps6[:, 0:1]).then_inc(s_pa, 1)
                    s.wait_ge(s_pp, NP * b + 3)
                    s.activation(xs[:], flat(pc).rearrange("p (k n) -> p k n", k=KC), ACT.Copy).then_inc(s_pa, 1)
                    s.activation(xT[:, :, bass.ds(b * P, P)], flat(pc).rearrange("p (k n) -> p k n", k=KC),
                                 ACT.Copy).then_inc(s_pa, 1)
                    s.wait_ge(s_pp, NP * b + 4)
                    s.activation(r1[:], flat(pa), ACT.Silu).then_inc(s_pa, 1)
                    s.wait_ge(s_pp, NP * b + 5)
                    s.wait_ge(s_pr, 16 * b)
                    s.activation(r2[:], flat(pb), ACT.Silu).then_inc(s_pa, 1)

            @block.tensor
            def _(t):
                t.wait_ge(s_pw, 48)
                with t.Fori(0, B) as b:
                    t.wait_ge(s_px, 16 * b + 16)
                    t.wait_ge(s_pa, NA * b)
                    for h in range(HALF):
                        last = t.matmul(pa[:, h], inv_c[:], xin[:, h * QW:(h + 1) * QW], start=True, stop=True)
                    last.then_inc(s_pp, 1)
                    for quad, e in edge_steps(b, 0, 1):
                        edges_tensor(t, quad, e)
                    t.wait_ge(s_pa, NA * b + 1)
                    for h in range(HALF):
                        last = t.matmul(pb[:, h], inv_c[:], sq[:, h * QW:(h + 1) * QW], start=True, stop=True)
                    last.then_inc(s_pp, 1)
                    for quad, e in edge_steps(b, 1, 2):
                        edges_tensor(t, quad, e)
                    t.wait_ge(s_pv, NV * b + 3)
                    for k in range(KC):
                        last = t.transpose(pc[:, k // 4, (k % 4) * P:(k % 4 + 1) * P], xc[:, k * P:(k + 1) * P],
                                           ident[:])
                    last.then_inc(s_pp, 1)
                    for quad, e in edge_steps(b, 2, 4):
                        edges_tensor(t, quad, e)
                    t.wait_ge(s_pa, NA * b + 3)
                    for h in range(HALF):
                        for k in range(KC):
                            t.matmul(pa[:, h], xs[:, k, :], w_spa[:, k, h * QW:(h + 1) * QW],
                                     start=(k == 0), stop=False)
                        last = t.matmul(pa[:, h], ones[0:1, :], b_spa[:, h * QW:(h + 1) * QW], start=False, stop=True)
                    last.then_inc(s_pp, 1)
                    for quad, e in edge_steps(b, 4, 6):
                        edges_tensor(t, quad, e)
                    t.wait_ge(s_pa, NA * b + 5)
                    for h in range(HALF):
                        last = t.matmul(pb[:, h], w_res[:], r1[:, h * QW:(h + 1) * QW], start=True, stop=True)
                    last.then_inc(s_pp, 1)
                    for quad, e in edge_steps(b, 6, QUADS_PRE * QC):
                        edges_tensor(t, quad, e)

            @block.gpsimd
            def _(g):
                edges_gpsimd(g, 0, B * QUADS_PRE)

        quads = B * QUADS_PRE
        for m in (1, 2):
            w = {k: a[f"m{m}_{k}"] for k in ("WinT", "convw", "convb", "WxT", "WdtT", "bdt", "Alog", "D", "WoutT")}
            n = f"_{m}"
            lstack = ExitStack()
            layer_sems = []

            def sem_l(name):
                layer_sems.append(nc.alloc_semaphore(name=name))
                return layer_sems[-1]

            conv_w = sb("conv_w" + n, [P, KC, DCONV], F32, lstack)
            conv_b = sb("conv_b" + n, [P, KC], F32, lstack)
            dt_b = sb("dt_b" + n, [P, KC], F32, lstack)
            rate = sb("rate" + n, [P, KC, NST], F32, lstack)
            skip = sb("skip" + n, [P, KC], F32, lstack)
            s_small = sem_l("s_small" + n)

            s_w = [sem_l(f"s_w{x}{n}") for x in range(2)]
            s_jdone = [sem_l(f"s_jdone{x}{n}") for x in range(2)]
            s_mm = [sem_l(f"s_mm{x}{n}") for x in range(2)]
            s_ev = [sem_l(f"s_ev{x}{n}") for x in range(2)]
            s_zev = [sem_l(f"s_zev{x}{n}") for x in range(2)]
            s_cv = [sem_l(f"s_cv{x}{n}") for x in range(2)]
            s_cch = sem_l("s_cch" + n)
            s_pad = sem_l("s_pad" + n)
            s_u = sem_l("s_u" + n)
            s_zs = [sem_l(f"s_zs{x}{n}") for x in range(2)]
            s_rate = sem_l("s_rate" + n)
            with ExitStack() as st, nc.Block() as block:
                raw = edges_buffer("in" + n, KC * QUADS_P1, st)
                w_in = big[:].rearrange("p k n -> p (k n)")[:, 0:4 * S].rearrange(
                    "p (x z k n) -> p x z k n", x=2, z=2, k=KC)
                w_x = sb("w_x" + n, [P, 2, XD], F32, st)
                padded = [sb(f"padded{x}{n}", [P, 4, P + DCONV - 1], F32, st) for x in range(2)]
                acc = [sb(f"acc{x}{n}", [P, 4, P], F32, st) for x in range(2)]
                zst = [sb(f"zst{x}{n}", [P, QW], F32, st) for x in range(2)]
                bank = [conv_ps[:, 4, :], conv_ps[:, 5, :]]
                JJ = KC // 2

                @block.sync
                def _(sp):
                    edges_load(sp, raw[0], quads + 1, KC * QUADS_P1)
                    for dst_, src_ in ((conv_w[:], w["convw"].rearrange("(k p) o t -> p k (o t)", p=P)),
                                       (conv_b[:], w["convb"].rearrange("(k p) -> p k", p=P)),
                                       (dt_b[:], w["bdt"].rearrange("(k p) -> p k", p=P)),
                                       (rate[:], w["Alog"].rearrange("(k p) t -> p k t", p=P)),
                                       (skip[:], w["D"].rearrange("(k p) -> p k", p=P))):
                        with nc.allow_non_contiguous_dma(reason="small parameters, one to a partition"):
                            sp.dma_start(dst_, src_).then_inc(s_small, 16)
                    with sp.Fori(0, JJ) as jj:
                        for x in range(2):
                            j = 2 * jj + x
                            sp.wait_ge(s_jdone[x], jj)
                            for z in range(2):
                                sp.dma_start(w_in[:, x, z], w["WinT"].rearrange("(k p) n -> p k n", p=P)
                                             [:, :, bass.ds(j * P + z * S, P)]).then_inc(s_w[x], 16)
                            sp.dma_start(w_x[:, x], w["WxT"][bass.ds(j * P, P), :]).then_inc(s_w[x], 16)
                            for q in range(NQ):
                                sp.wait_ge(s_zev[q % 2], 4 * jj + 2 * x + q // 2 + 1)
                                sp.dma_start(sz_d[bass.ds(j, 1), :, q * QW:(q + 1) * QW]
                                             .rearrange("o p n -> (o p) n"), zst[q % 2][:]).then_inc(s_zs[q % 2], 16)
                    for x in range(2):
                        sp.wait_ge(s_zs[x], 16 * KC * 2)

                @block.vector
                def _(v):
                    for x in range(2):
                        v.memset(padded[x][:], 0.0).then_inc(s_pad, 1)
                    v.wait_ge(s_small, 80)
                    with v.Fori(0, KC) as j:
                        ck = Chain(v, s_cch, 8 * j)
                        for z in range(2):
                            for q in range(NQ):
                                edges_vector(v, quads + 2 * j + z, q, raw, 2 * j + z)
                                if z:
                                    continue
                                x = q % 2
                                v.wait_ge(s_ev[x], 2 * j + q // 2 + 1)
                                for tap in (2, 1, 0):
                                    op = v.scalar_tensor_tensor(
                                        out=acc[x][:], in0=padded[x][:, :, tap:tap + P],
                                        scalar=conv_w[:, bass.ds(j, 1), tap:tap + 1].rearrange("p k t -> p (k t)"),
                                        in1=acc[x][:], op0=ALU.mult, op1=ALU.add)
                                    if tap:
                                        ck(op)
                                    else:
                                        op.then_inc(s_cv[x], 1)
                        ck.end(8)

                @block.scalar
                def _(s):
                    s.wait_ge(s_pad, 2)
                    s.wait_ge(s_small, 80)
                    with s.Fori(0, KC) as j:
                        def evacuate(q):
                            x = q % 2
                            s.wait_ge(s_mm[x], 4 * j + q // 2 + 1)
                            s.wait_ge(s_cv[x], 2 * j + q // 2)
                            s.wait_ge(s_u, 4 * j + max(q - 1, 0))
                            src = bank[x].rearrange("p (b n) -> p b n", n=P)
                            s.activation(padded[x][:, :, DCONV - 1:], src, ACT.Copy)
                            s.activation(acc[x][:], src, ACT.Identity, bias=conv_b[:, bass.ds(j, 1)],
                                         scale=conv_w[:, bass.ds(j, 1), 3:4].rearrange("p k t -> p (k t)"))\
                                .then_inc(s_ev[x], 1)

                        def gate(q):
                            x = q % 2
                            wait_apart(s, (s_cv[x], 2 * j + q // 2 + 1))
                            s.activation(act[:, bass.ds(j, 1), q * QW:(q + 1) * QW],
                                         acc[x][:].rearrange("p b n -> p (b n)").unsqueeze(1),
                                         ACT.Silu).then_inc(s_u, 1)

                        evacuate(0)
                        for q in range(1, NQ):
                            evacuate(q)
                            gate(q - 1)
                        gate(NQ - 1)
                        for q in range(NQ):
                            x = q % 2
                            s.wait_ge(s_mm[x], 4 * j + 2 + q // 2 + 1)
                            s.wait_ge(s_zs[x], 32 * j + 16 * (q // 2))
                            s.activation(zst[x][:], bank[x], ACT.Silu).then_inc(s_zev[x], 1)
                    s.activation(rate[:], rate[:], ACT.Exp).then_inc(s_rate, 1)
                    s.wait_ge(s_rate, 1)
                    s.mul(rate[:], rate[:], -1.0).then_inc(s_rate, 1)

                @block.tensor
                def _(t):
                    t.wait_ge(s_pad, 2)
                    for q in range(NQ):
                        t.matmul(conv_ps[0:XD, q, :], padded[0][:, 0, 0:XD],
                                 padded[0][:].rearrange("p b n -> p (b n)")[:, 0:QW], start=True, stop=True)
                    with t.Fori(0, JJ) as jj:
                        for x_ in range(2):
                            t.wait_ge(s_w[x_], 48 * jj + 48)
                            for z in range(2):
                                for q in range(NQ):
                                    x = q % 2
                                    if z == 0 and q < 2:
                                        t.wait_ge(s_zev[x], 4 * jj + 2 * x_)
                                    elif z == 0:
                                        t.wait_ge(s_ev[x], 4 * jj + 2 * x_ + 1)
                                    elif q < 2:
                                        t.wait_ge(s_ev[x], 4 * jj + 2 * x_ + 2)
                                    else:
                                        t.wait_ge(s_zev[x], 4 * jj + 2 * x_ + 1)
                                    for k in range(KC):
                                        last = t.matmul(bank[x], w_in[:, x_, z, k, :],
                                                        xT[:, k, q * QW:(q + 1) * QW],
                                                        start=(k == 0), stop=(k == KC - 1))
                                    last.then_inc(s_mm[x], 1)
                                    edges_tensor(t, quads + 2 * (2 * jj + x_) + z, q)
                            for q in range(NQ):
                                t.wait_ge(s_u, 8 * jj + 4 * x_ + q + 1)
                                last = t.matmul(conv_ps[0:XD, q, :], w_x[:, x_, :],
                                                act[:, bass.ds(2 * jj + x_, 1), q * QW:(q + 1) * QW],
                                                start=False, stop=True, skip_group_check=True)
                            last.then_inc(s_jdone[x_], 1)

                @block.gpsimd
                def _(g):
                    edges_gpsimd(g, quads, KC * QUADS_P1)
            quads += KC * QUADS_P1

            s_dbl = sem_l("s_dbl" + n)
            s_sp2 = sem_l("s_spread" + n)
            s_spev = sem_l("s_spev" + n)
            s_wdt = [sem_l(f"s_wdt{x}{n}") for x in range(2)]
            s_dtmm = [sem_l(f"s_dtmm{x}{n}") for x in range(2)]
            s_soft = [sem_l(f"s_soft{x}{n}") for x in range(2)]
            s_ach = sem_l("s_ach" + n)
            s_dt = [sem_l(f"s_dt{x}{n}") for x in range(2)]
            s_decay = [sem_l(f"s_decay{x}{n}") for x in range(2)]
            s_gz = [sem_l(f"s_gz{x}{n}") for x in range(2)]
            s_y = [sem_l(f"s_y{x}{n}") for x in range(2)]
            s_vch = sem_l("s_vch" + n)
            with ExitStack() as st, nc.Block() as block:
                dbl = sb("dbl" + n, [XD, NT], F32, st)
                raw = edges_buffer("scan" + n, KC * QUADS_P2, st)
                w_dt = sb("w_dt" + n, [DTR, 2, P], F32, st)
                free = xT[:].rearrange("p k (c n) -> p (k c) n", n=QW)
                soft, relu, dec0, dec1, gz, dtu, h0, h1 = ([free[:, 2 * i + x, :] for x in range(2)] for i in range(8))
                bank = [conv_ps[:, 4, :], conv_ps[:, 5, :]]
                JJ = KC // 2

                @block.sync
                def _(sp):
                    edges_load(sp, raw[0], quads + 1, KC * QUADS_P2)
                    with sp.Fori(0, JJ) as jj:
                        for x_ in range(2):
                            j = 2 * jj + x_
                            for q in range(NQ):
                                x = q % 2
                                sp.wait_ge(s_y[x], 4 * jj + 2 * x_ + q // 2)
                                if q == 1:
                                    sp.dma_start(w_dt[:, x_], w["WdtT"][:, bass.ds(j * P, P)]).then_inc(s_wdt[x_], 16)
                                sp.dma_start(gz[x], sz_d[bass.ds(j, 1), :, q * QW:(q + 1) * QW]
                                             .rearrange("o p n -> (o p) n")).then_inc(s_gz[x], 16)

                @block.tensor
                def _(t):
                    t.wait_ge(s_dbl, 1)
                    for r in range(2 * NST):
                        for q in range(NQ):
                            i = r * NQ + q
                            if i >= 2:
                                t.wait_ge(s_spev, i - 1)
                            t.matmul(bank[i % 2], ident[0:XD, DTR + r:DTR + r + 1].to_broadcast([XD, P]),
                                     dbl[:, q * QW:(q + 1) * QW], start=True, stop=True).then_inc(s_sp2, 1)
                    t.wait_ge(s_spev, 4 * NQ)
                    with t.Fori(0, JJ) as jj:
                        for x_ in range(2):
                            t.wait_ge(s_wdt[x_], 16 * jj + 16)

                            def dt_product(q):
                                x = q % 2
                                t.wait_ge(s_soft[x], 4 * jj + 2 * x_ + q // 2)
                                t.matmul(bank[x], w_dt[:, x_, :], dbl[0:DTR, q * QW:(q + 1) * QW],
                                         start=True, stop=True).then_inc(s_dtmm[x], 1)

                            dt_product(0)
                            for q in range(NQ):
                                if q + 1 < NQ:
                                    dt_product(q + 1)
                                for e in range(QUADS_P2 * q, QUADS_P2 * (q + 1)):
                                    edges_tensor(t, quads + (2 * jj + x_) * QUADS_P2 + e // QC, e % QC)

                @block.scalar
                def _(s):
                    s.activation(dbl[:].rearrange("p (q n) -> p q n", q=NQ), conv_ps[0:XD, 0:NQ, :],
                                 ACT.Copy).then_inc(s_dbl, 1)
                    for i in range(2 * NST * NQ):
                        s.wait_ge(s_sp2, i + 1)
                        s.activation(big[:, i // NQ, (i % NQ) * QW:(i % NQ + 1) * QW], bank[i % 2],
                                     ACT.Copy).then_inc(s_spev, 1)
                    with s.Fori(0, KC) as j:
                        ck = Chain(s, s_ach, 2 * NQ * j)

                        def softplus(q):
                            x = q % 2
                            wait_apart(s, (s_dtmm[x], 2 * j + q // 2 + 1), (s_y[x], 2 * j + q // 2))
                            bias = dt_b[:, bass.ds(j, 1)]
                            s.activation(relu[x], bank[x], ACT.Relu, bias=bias)
                            ck(s.activation(soft[x], bank[x], ACT.Abs, bias=bias))
                            ck(s.activation(soft[x], soft[x], ACT.Exp, scale=-1.0))
                            s.activation(soft[x], soft[x], ACT.Ln, bias=1.0).then_inc(s_soft[x], 1)

                        def decay(q):
                            x = q % 2
                            wait_apart(s, (s_dt[x], 2 * j + q // 2 + 1))
                            for i, d in enumerate((dec0, dec1)):
                                last = s.activation(d[x], soft[x], ACT.Exp,
                                                    scale=rate[:, bass.ds(j, 1), i:i + 1].rearrange("p k t -> p (k t)"))
                            last.then_inc(s_decay[x], 1)

                        softplus(0)
                        for q in range(1, NQ):
                            softplus(q)
                            decay(q - 1)
                        decay(NQ - 1)
                        ck.end(2 * NQ)

                @block.vector
                def _(v):
                    VCK = 8 * NQ
                    with v.Fori(0, KC) as j:
                        ck = Chain(v, s_vch, VCK * j)

                        def edges(e):
                            edges_vector(v, quads + j * QUADS_P2 + e // QC, e % QC, raw, j * QUADS_P2 + e // QC)

                        for q in range(NQ):
                            x = q % 2
                            cols = slice(q * QW, (q + 1) * QW)
                            u = act[:, bass.ds(j, 1), cols].rearrange("p k n -> p (k n)")
                            bm0, bm1, cm0, cm1 = (big[:, i, cols] for i in range(4))
                            v.wait_ge(s_soft[x], 2 * j + q // 2 + 1)
                            v.tensor_tensor(soft[x], soft[x], relu[x], ALU.add).then_inc(s_dt[x], 1)
                            edges(2 * q)
                            v.wait_ge(s_dt[x], 2 * j + q // 2 + 1)
                            ck(v.tensor_tensor(dtu[x], soft[x], u, ALU.mult))
                            v.tensor_tensor(h0[x], dtu[x], bm0, ALU.mult)
                            ck(v.tensor_tensor(h1[x], dtu[x], bm1, ALU.mult))
                            v.wait_ge(s_decay[x], 2 * j + q // 2 + 1)
                            for d in (dec0, dec1):
                                op = v.memset(d[x].rearrange("p (b n) -> p b n", n=P)[:, :, 0:1], 0.0)
                            ck(op)
                            v.tensor_tensor_scan(h0[x], dec0[x], h0[x], 0.0, ALU.mult, ALU.add)
                            scanned = ck.mark(v.tensor_tensor_scan(h1[x], dec1[x], h1[x], 0.0, ALU.mult, ALU.add))
                            edges(2 * q + 1)
                            ck.wait(scanned)
                            v.tensor_tensor(h0[x], h0[x], cm0, ALU.mult)
                            ck(v.tensor_tensor(h1[x], h1[x], cm1, ALU.mult))
                            ck(v.tensor_tensor(h0[x], h0[x], h1[x], ALU.add))
                            ck(v.scalar_tensor_tensor(out=h0[x], in0=u, scalar=skip[:, bass.ds(j, 1)], in1=h0[x],
                                                      op0=ALU.mult, op1=ALU.add))
                            v.wait_ge(s_gz[x], 32 * j + 16 * (q // 2) + 16)
                            ck(v.tensor_tensor(u, h0[x], gz[x], ALU.mult))
                            v.sem_inc(s_y[x], 1)
                        ck.end(8 * NQ)

                @block.gpsimd
                def _(g):
                    edges_gpsimd(g, quads, KC * QUADS_P2)
            quads += KC * QUADS_P2

            s_wo = sem_l("s_wo" + n)
            s_gb = sem_l("s_gb" + n)
            s_oa = sem_l("s_oa" + n)
            s_op = sem_l("s_op" + n)
            s_ov = sem_l("s_ov" + n)
            s_ox = sem_l("s_ox" + n)
            with ExitStack() as st, nc.Block() as block:
                raw = edges_buffer("out" + n, B, st)
                if m == 2:
                    raw = (raw[0], raw[1] + 1)
                ys = sb("ys" + n, [P, KC, P], F32, st)
                sn = sb("sn" + n, [P, S], F32, st)
                ln_g = sb("ln_g" + n, [P, S], F32, st)
                ln_b = sb("ln_b" + n, [P, S], F32, st)
                stats = sb("stats" + n, [P, HALF, 6], F32, st)
                mv = sb("mv" + n, [P, 2], F32, st)
                dev = sb("dev" + n, [P, 1], F32, st)
                rstd = sb("rstd" + n, [P, 1], F32, st)
                w_mid = sb("w_mid" + n, [P, P], F32, st)
                rb = sb("rb" + n, [P, S], F32, st)
                xb = sb("xb" + n, [P, S], F32, st)
                w_out = big[:].rearrange("p k n -> p (k n)").rearrange("p (k n) -> p k n", k=KC)
                po, pt = conv_ps[:, 0:2, :], conv_ps[:, 2:4, :]
                NA, NP, NV = 3, 2 if m == 1 else 1, 8 if m == 1 else 10

                @block.sync
                def _(sp):
                    if m == 1:
                        edges_load(sp, raw[0], quads + 1, B)
                    else:
                        edges_load(sp, raw[0], quads + 1, B - 1)
                        edges_load(sp, raw[0][:, :, B - 1:B, :], quads, 1)
                    sp.dma_start(w_out, w["WoutT"].rearrange("(k p) n -> p k n", p=P)).then_inc(s_wo, 16)
                    sp.dma_start(ln_g[:], a[f"ln{m}_g"].rearrange("(o n) -> o n", o=1).partition_broadcast(P)
                                 .rearrange("p o n -> p (o n)")).then_inc(s_gb, 16)
                    sp.dma_start(ln_b[:], a[f"ln{m}_b"].rearrange("(o n) -> o n", o=1).partition_broadcast(P)
                                 .rearrange("p o n -> p (o n)")).then_inc(s_gb, 16)
                    if m == 1:
                        sp.dma_start(w_mid[:], a["w_midT"]).then_inc(s_wo, 16)
                    else:
                        with sp.Fori(0, B) as b:
                            sp.wait_ge(s_ov, NV * b)
                            sp.dma_start(rb[:], r_d[bass.ds(b, 1)].rearrange("o c s -> (o c) s")).then_inc(s_ox, 16)
                            sp.dma_start(xb[:], x_in[bass.ds(b, 1)].rearrange("o c s -> (o c) s")).then_inc(s_ox, 16)

                @block.scalar
                def _(s):
                    with s.Fori(0, B) as b:
                        wait_apart(s, (s_op, NP * b))
                        s.activation(ys[:], act[:, :, bass.ds(b * P, P)], ACT.Copy).then_inc(s_oa, 1)
                        s.wait_ge(s_ov, NV * b + 3)
                        s.activation(dev[:], mv[:, 1:2], ACT.Sqrt, bias=eps5[:, 0:1]).then_inc(s_oa, 1)
                        if m == 1:
                            wait_apart(s, (s_op, NP * b + 2))
                            s.activation(xT[:, :, bass.ds(b * P, P)],
                                         pt.rearrange("p h n -> p (h n)").rearrange("p (k n) -> p k n", k=KC),
                                         ACT.Silu).then_inc(s_oa, 1)
                        else:
                            s.wait_ge(s_ov, NV * b + 8)
                            s.activation(rb[:], rb[:], ACT.Silu).then_inc(s_oa, 1)

                @block.tensor
                def _(t):
                    t.wait_ge(s_wo, 32 if m == 1 else 16)
                    with t.Fori(0, B) as b:
                        t.wait_ge(s_oa, NA * b + 1)
                        t.wait_ge(s_ov, NV * b)
                        for h in range(HALF):
                            for k in range(KC):
                                last = t.matmul(po[:, h], ys[:, k, :], w_out[:, k, h * QW:(h + 1) * QW],
                                                start=(k == 0), stop=(k == KC - 1))
                            if h:
                                last.then_inc(s_op, 1)
                            edges_tensor(t, quads + b, h)
                        edges_tensor(t, quads + b, 2)
                        if m == 1:
                            t.wait_ge(s_ov, NV * b + NV)
                            t.wait_ge(s_oa, NA * b)
                            for k in range(KC):
                                last = t.matmul(pt[:, k // 4, (k % 4) * P:(k % 4 + 1) * P], sn[:, k * P:(k + 1) * P],
                                                w_mid[:], start=True, stop=True)
                            last.then_inc(s_op, 1)
                        edges_tensor(t, quads + b, 3)

                @block.vector
                def _(v):
                    v.wait_ge(s_gb, 32)
                    with v.Fori(0, B) as b:
                        ck = Chain(v, s_ov, NV * b)
                        edges_vector(v, quads + b, 0)
                        edges_vector(v, quads + b, 1)
                        v.wait_ge(s_op, NP * b + 1)
                        for h in range(HALF):
                            ck(v.bn_stats(stats[:, h, :], po[:, h]), wait_apart)
                        ck(v.bn_aggr(mv[:], stats[:].rearrange("p h n -> p (h n)")))
                        v.wait_ge(s_oa, NA * b + 2)
                        ck(v.reciprocal(rstd[:], dev[:]))
                        if m == 1:
                            v.wait_ge(s_op, NP * b)
                        ck(v.tensor_scalar(sn[:], po.rearrange("p h n -> p (h n)"), mv[:, 0:1], rstd[:, 0:1],
                                           ALU.subtract, ALU.mult))
                        ck(v.tensor_tensor(sn[:], sn[:], ln_g[:], ALU.mult))
                        ck(v.tensor_tensor(sn[:], sn[:], ln_b[:], ALU.add))
                        if m == 1:
                            v.sem_inc(s_ov, 1)
                        else:
                            v.wait_ge(s_ox, 32 * b + 32)
                            ck(v.tensor_tensor(rb[:], sn[:], rb[:], ALU.add))
                            v.wait_ge(s_oa, NA * b + 3)
                            ck(v.tensor_tensor(x2[:, bass.ds(b * S, S)], rb[:], xb[:], ALU.add))
                            v.sem_inc(s_ov, 1)
                        edges_vector(v, quads + b, 2)
                        edges_vector(v, quads + b, 3, raw, b)

                @block.gpsimd
                def _(g):
                    edges_gpsimd(g, quads, B * QUADS_OUT)
            quads += B * QUADS_OUT
            lstack.close()
            nc.clear_and_free_semaphores(layer_sems)
            nc.all_engine_barrier()
        assert quads == QUADS, quads
        mstack.close()
        estack.close()

        a_dst = sb("a_dst", [P, BINS, HEADS], F32)
        peak = sb("peak", [P, BINS, HEADS], F32)
        total = sb("total", [P, BINS, HEADS, EXP + 1], F32)
        bins_sb = sb("bins_sb", [1, CHUNKS + 1], I32)
        H16 = HEADS * EXP
        SPLIT = 2 * (H16 + HEADS)
        NSP = 3 * HEADS

        s_tw = sem("s_tw")
        s_tz = sem("s_tz")
        s_tv = sem("s_tv")
        s_ta = sem("s_ta")
        s_tp = sem("s_tp")
        s_tab = sem("s_tab")
        with ExitStack() as st, nc.Block() as block:
            stat_ps = ps("stat_ps", [P, 2, HALF, QW], F32, st)
            h_ps = ps("h_ps", [P, KC, H16], F32, st)
            tn = sb("tn", [P, S], F32, st)
            dv = sb("dv", [P, S], F32, st)
            rows = sb("rows", [P, KC, ROW], F32, st)
            rows_b = rows[:].rearrange("p t f -> p (t f)").bitcast(BF16).rearrange("p (t f) -> p t f", f=2 * ROW)
            weighed = sb("weighed", [P, KC, HEADS, EXP], F32, st)
            weighed2 = sb("weighed2", [P, KC, HEADS, EXP], F32, st)
            rest = sb("rest", [P, KC, HEADS], F32, st)
            logit = sb("logit", [P, KC, HEADS], F32, st)
            w_gat = sb("w_gat", [P, H16], F32, st)
            att_s = sb("att_s", [P, H16], F32, st)
            att_d = sb("att_d", [P, H16], F32, st)
            zrow = sb("zrow", [1, ROW], F32, st)
            mean_ps, var_ps = (stat_ps[:, i].rearrange("p h n -> p (h n)") for i in range(2))
            NV, NA, NP = 15, 3, 3
            full = [P, KC, HEADS, EXP]

            @block.sync
            def _(sp):
                for n in range(QC):
                    sp.wait_ge(s_scat[n], 16 * CH * QUADS)
                sp.dma_start(w_gat[:], a["W_gat"]).then_inc(s_tw, 16)
                for to, name in ((att_s, "att_src"), (att_d, "att_dst")):
                    sp.dma_start(to[:], a[name].rearrange("(o h) e -> o (h e)", o=1).partition_broadcast(P)
                                 .rearrange("p o n -> p (o n)")).then_inc(s_tw, 16)
                sp.dma_start(bins_sb[:], scr["bins"]).then_inc(s_tw, 16)
                sp.wait_ge(s_tz, 2)
                sp.dma_start(tab_d[M:M + 1, :], zrow[:]).then_inc(s_tab, 16)
                with sp.Fori(0, B) as b:
                    sp.wait_ge(s_tv, NV * b + 13)
                    sp.dma_start(tab_d[bass.ds(b * S, S), :].rearrange("(t p) f -> p t f", p=P),
                                 rows[:]).then_inc(s_tab, 16)
                sp.wait_ge(s_tab, 16 * B + 16)

            @block.vector
            def _(v):
                v.memset(rows[:], 0.0).then_inc(s_tz, 1)
                v.memset(zrow[:], 0.0).then_inc(s_tz, 1)
                v.wait_ge(s_tz, 2)
                v.wait_ge(s_tw, 64)
                with v.Fori(0, B) as b:
                    ck = Chain(v, s_tv, NV * b)
                    tiles = bass.ds(b * KC, KC)
                    v.wait_ge(s_tp, NP * b + 1)
                    v.wait_ge(s_ta, NA * b)
                    ck(v.tensor_tensor(tn[:], x2[:, bass.ds(b * S, S)], mean_ps, ALU.subtract))
                    v.wait_ge(s_ta, NA * b + 2)
                    ck(v.reciprocal(dv[:], dv[:]))
                    ck(v.tensor_tensor(tn[:], tn[:], dv[:], ALU.mult))
                    v.wait_ge(s_tp, NP * b + 3)
                    v.wait_ge(s_tab, 16 * b + 16)
                    h_view = rows[:, :, 0:H16].rearrange("p t (h e) -> p t h e", e=EXP)
                    src_log = rows[:, :, H16:H16 + HEADS]
                    ck(v.tensor_copy(rows[:, :, 0:H16], h_ps[:]))
                    for att, prod_ in ((att_s, weighed), (att_d, weighed2)):
                        op = v.tensor_tensor(prod_[:], h_view, att[:].rearrange("p (h e) -> p h e", e=EXP)
                                             .unsqueeze(1).to_broadcast(full), ALU.mult)
                    ck(op)
                    v.tensor_reduce(src_log, weighed[:], AX.X, ALU.add)
                    ck(v.tensor_reduce(a_dst[:, tiles, :], weighed2[:], AX.X, ALU.add))
                    part = [rows_b[:, :, SPLIT + HEADS * i:SPLIT + HEADS * (i + 1)] for i in range(3)]
                    ck(v.tensor_copy(part[0], src_log))
                    ck(v.tensor_tensor(rest[:], src_log, part[0], ALU.subtract))
                    ck(v.tensor_copy(part[1], rest[:]))
                    ck(v.tensor_tensor(rest[:], rest[:], part[1], ALU.subtract))
                    ck(v.tensor_copy(part[2], rest[:]))
                    ck(v.tensor_tensor(logit[:], src_log, a_dst[:, tiles, :], ALU.add), wait_apart)
                    v.tensor_copy(total[:, tiles, :, 0:EXP], h_view)
                    ck(v.tensor_copy(total[:, tiles, :, EXP], ones[:, 0:KC * HEADS].rearrange("p (t h) -> p t h", t=KC)))
                    ck(v.scalar_tensor_tensor(out=peak[:, tiles, :], in0=logit[:], scalar=0.2, in1=logit[:],
                                              op0=ALU.mult, op1=ALU.max))
                    v.sem_inc(s_tv, 1)
                    ck.end(NV - 1)

            @block.scalar
            def _(s):
                with s.Fori(0, B) as b:
                    s.wait_ge(s_tv, NV * b + 1)
                    s.activation(dv[:], tn[:], ACT.Square).then_inc(s_ta, 1)
                    s.wait_ge(s_tp, NP * b + 2)
                    s.wait_ge(s_ta, NA * b + 1)
                    s.activation(dv[:], var_ps, ACT.Sqrt, bias=eps5[:, 0:1]).then_inc(s_ta, 1)
                    wait_apart(s, (s_tv, NV * b + 3))
                    s.activation(tokens[:, bass.ds(b * S, S)], tn[:], ACT.Copy).then_inc(s_ta, 1)

            @block.tensor
            def _(t):
                t.wait_ge(s_tw, 64)
                with t.Fori(0, B) as b:
                    t.wait_ge(s_tv, NV * b)
                    for h in range(HALF):
                        last = t.matmul(stat_ps[:, 0, h], inv_c[:], x2[:, bass.ds(b * S + h * QW, QW)],
                                        start=True, stop=True)
                    last.then_inc(s_tp, 1)
                    t.wait_ge(s_ta, NA * b + 1)
                    for h in range(HALF):
                        last = t.matmul(stat_ps[:, 1, h], inv_c[:], dv[:, h * QW:(h + 1) * QW],
                                        start=True, stop=True)
                    last.then_inc(s_tp, 1)
                    t.wait_ge(s_tv, NV * b + 3)
                    for k in range(KC):
                        last = t.matmul(h_ps[:, k, :], tn[:, k * P:(k + 1) * P], w_gat[:], start=True, stop=True)
                    last.then_inc(s_tp, 1)

        LOAD, FETCH, SPREAD, MAX, WEIGH = 6, 5, 3, 2, 1
        s_sel = sem("s_sel")
        s_pk = [sem(f"s_pk{x}") for x in range(SL)]
        s_gat = [sem(f"s_gat{x}") for x in range(SL)]
        s_src = sem("s_src")
        s_lo = sem("s_lo")
        s_far = sem("s_far")
        s_oh = sem("s_oh")
        s_otp = sem("s_otp")
        s_ot = sem("s_ot")
        s_stp = sem("s_stp")
        s_spl = sem("s_spl")
        s_bc = sem("s_bc")
        s_cmax = sem("s_cmax")
        s_max = sem("s_max")
        s_resc = sem("s_resc")
        s_pg = sem("s_pg")
        s_q = sem("s_q")
        s_wgt = sem("s_wgt")
        s_msg = sem("s_msg")
        s_pa2 = sem("s_pa2")
        s_sum = sem("s_sum")
        s_gch = sem("s_gch")
        with ExitStack() as st, nc.Block() as block:
            NPART = 3
            TS, MS, RS = 4, 2, 4
            packed = sb("packed", [P, SL, EC], I32, st)
            src_i = sb("src_i", [P, SL, EC], I32, st)
            lo_i = sb("lo_i", [P, EC], I32, st)
            lo_f = sb("lo_f", [P, 2, EC], F32, st)
            apart = sb("apart", [P, EC, P], F32, st)
            got = sb("got", [P, SL, EC, ROW], F32, st)
            pick = sb("pick", [P, SL, EC, P], F32, st)
            pickT = sb("pickT", [P, TS, CE], BF16, st)
            away = sb("away", [P, TS, CE], F32, st)
            split = sb("split", [NSP, CE], BF16, st)
            sel3 = sb("sel3", [NSP, HEADS, P], BF16, st)
            junk = sb("junk", [P, HEADS, CE], F32, st)
            cmax = sb("cmax", [P, HEADS], F32, st)
            edge_l = sb("edge_l", [P, HEADS], F32, st)
            leak = sb("leak", [P, HEADS], F32, st)
            node = sb("node", [P, 2 * HEADS], F32, st)
            node_b = sb("node_b", [P, 2, NPART, 2 * HEADS], BF16, st)
            rem = sb("rem", [P, 2 * HEADS], F32, st)
            rem2 = sb("rem2", [P, 2 * HEADS], F32, st)
            node_e = sb("node_e", [P, EC, 2 * HEADS], F32, st)
            fall = sb("fall", [P, HEADS], F32, st)
            resc = sb("resc", [P, RS, HEADS], F32, st)
            zl = sb("zl", [P, EC, HEADS], F32, st)
            zk = sb("zk", [P, EC, HEADS], F32, st)
            zq = sb("zq", [P, EC, HEADS], F32, st)
            msg = sb("msg", [P, MS, EC, HEADS, EXP + 1], F32, st)
            far_b = sb("far_b", [P, 1], F32, st)
            pickT_ps = ps("pickT_ps", [P, CE], F32, st)
            bc_ps = ps("bc_ps", [P, HEADS, CE], F32, st)
            split_ps = ps("split_ps", [P, 2 * QW], BF16, st)
            node_ps = ps("node_ps", [P, QW], F32, st)
            sum_ps = ps("sum_ps", [P, QW], F32, st)
            node_v = node_ps[:, 0:EC * NPART * 2 * HEADS].rearrange("p (t x) -> p t x", t=EC)
            sum_v = sum_ps[:, 0:HEADS * (EXP + 1)]

            def rounds(eng):
                return eng.value_load(bins_sb[0:1, CHUNKS:CHUNKS + 1], min_val=1, max_val=(CHUNKS - 8) // SL)

            def run(eng, step):
                for d in range(-FETCH, 0):
                    step(0, d)
                with eng.Fori(0, rounds(eng)) as i:
                    for d in range(SL):
                        step(i, d)

            def has(i, d):
                return not isinstance(i, int) or d >= 0

            @block.sync
            def _(sp):
                def load(i, d):
                    sp.dma_start(packed[:, d % SL, :], slots_d[bass.ds((i * SL + d) * CE, CE), :]
                                 .rearrange("(p f) o -> p (f o)", p=P)).then_inc(s_pk[d % SL], 16)

                def step(i, d):
                    if has(i, d):
                        sp.wait_ge(s_src, SL * i + d)
                    load(i, d + LOAD)

                load(0, 0)
                run(sp, step)

            @block.gpsimd
            def _(g):
                g.memset(sel3[:], 0.0).then_inc(s_sel, 1)
                g.memset(far_b[:], -BIG).then_inc(s_sel, 1)
                for k in range(3):
                    g.wait_ge(s_sel, 2 + k)
                    g.affine_select(out=sel3[:], in_=sel3[:], compare_op=ALU.not_equal, fill=1.0, base=-HEADS * k,
                                    pattern=[[-1, HEADS], [0, P]], channel_multiplier=1).then_inc(s_sel, 1)

                def step(i, d):
                    d += FETCH
                    wait_apart(g, (s_src, SL * i + d + 1))
                    for t in range(EC):
                        g.indirect_dma_start(got[:, d % SL, t, :], None, tab_d[:, :],
                                             bass.IndirectOffsetOnAxis(ap=src_i[:, d % SL, t:t + 1], axis=0))\
                            .then_inc(s_gat[d % SL], 16)

                run(g, step)

            @block.vector
            def _(v):
                bins = {}
                handed = [v.alloc_register(f"bin{x}") for x in range(MAX + 1)]

                def load_bin(i, d):
                    bins[d] = v.value_load(bins_sb[0:1, bass.ds(i * SL + d, 1)], min_val=0, max_val=BINS - 1)

                def hand_on(first):
                    for x, reg in enumerate(handed):
                        v.reg_mov(reg, bins[first + x])

                def take_over():
                    for x, reg in enumerate(handed):
                        bins[x] = bass.RuntimeValue.of_register_unchecked(reg, min_val=0, max_val=BINS - 1)

                def at_bin(state, d):
                    return [x[:, bass.ds(bins[d], 1)] for x in state]

                def step(i, u, ck):
                    c = SL * i + u
                    mx, wg, sm = has(i, u + MAX), has(i, u + WEIGH), has(i, u)
                    xm, xw, xf = (u + MAX) % SL, (u + WEIGH) % SL, (u + FETCH) % SL
                    start = ck.n
                    if mx:
                        ad, pk = (x.rearrange("p b h -> p (b h)") for x in at_bin((a_dst, peak), u + MAX))
                        wait_apart(v, (ck.sem, ck.base + start), (s_ot, c + MAX + 1), (s_bc, c + MAX + 1))
                        for h in range(HEADS):
                            v.tensor_tensor_reduce(junk[:, h, :], away[:, xm % TS, :], bc_ps[:, h, :], 1.0, -BIG,
                                                   ALU.add, ALU.max, cmax[:, h:h + 1]).then_inc(s_cmax, 1)
                        v.tensor_copy(node[:, 0:HEADS], ad)
                    if has(i, u + MAX + 1):
                        load_bin(i, u + MAX + 1)
                    if wg:
                        v.wait_ge(s_pg, c + WEIGH + 1)
                        l0 = ck.mark(v.tensor_reduce(node_e[:], node_v.rearrange("p t (k f) -> p t f k", k=NPART),
                                                     AX.X, ALU.add))
                    if mx:
                        wait_apart(v, (s_cmax, HEADS * (c + MAX + 1)))
                        m1 = ck.mark(v.tensor_tensor(edge_l[:], cmax[:], ad, ALU.add))
                    if wg:
                        ck.wait(l0)
                        l1 = ck.mark(v.tensor_tensor(zl[:], got[:, xw, :, H16:H16 + HEADS], node_e[:, :, 0:HEADS],
                                                     ALU.add))
                    if mx:
                        ck.wait(m1)
                        m2 = ck.mark(v.scalar_tensor_tensor(out=leak[:], in0=edge_l[:], scalar=0.2, in1=edge_l[:],
                                                            op0=ALU.mult, op1=ALU.max))
                    if wg:
                        ck.wait(l1)
                        l2 = ck.mark(v.scalar_tensor_tensor(out=zk[:], in0=zl[:], scalar=0.2, in1=zl[:],
                                                            op0=ALU.mult, op1=ALU.max))
                    if mx:
                        ck.wait(m2)
                        m3 = ck.mark(v.tensor_tensor(node[:, HEADS:], leak[:], pk, ALU.max))
                    if wg:
                        ck.wait(l2)
                        v.tensor_tensor(zq[:], zk[:], node_e[:, :, HEADS:], ALU.subtract).then_inc(s_q, 1)
                    part = [node_b[:, xm % 2, k, :] for k in range(NPART)]
                    if mx:
                        ck.wait(m3)
                        m4 = ck.mark(v.tensor_copy(part[0], node[:]))
                        if has(i, u + MAX - 1):
                            v.wait_ge(s_resc, c + MAX)
                        m5 = ck.mark(v.tensor_tensor(fall[:], pk, node[:, HEADS:], ALU.subtract))
                    if sm:
                        tot_, = (x.rearrange("p b h e -> p (b h) e") for x in at_bin((total,), u))
                        v.wait_ge(s_pa2, c + 1)
                        v.wait_ge(s_sum, c)
                        t1 = ck.mark(v.tensor_tensor(tot_, tot_, resc[:, u % RS, :].unsqueeze(2)
                                                     .to_broadcast([P, HEADS, EXP + 1]), ALU.mult))
                    if mx:
                        ck.wait(m4)
                        m6 = ck.mark(v.tensor_tensor(rem[:], node[:], part[0], ALU.subtract))
                    if sm:
                        ck.wait(t1)
                        v.tensor_tensor(tot_, tot_, sum_v.rearrange("p (h e) -> p h e", h=HEADS),
                                        ALU.add).then_inc(s_sum, 1)
                    if mx:
                        ck.wait(m6)
                        m7 = ck.mark(v.tensor_copy(part[1], rem[:]))
                    v.wait_ge(s_pk[xf], 16 * (i + (u + FETCH) // SL) + 16)
                    u1 = ck.mark(v.tensor_scalar(lo_i[:], packed[:, xf, :], SRC_BITS, None, ALU.logical_shift_right))
                    v.tensor_scalar(src_i[:, xf, :], packed[:, xf, :], (1 << SRC_BITS) - 1, None,
                                    ALU.bitwise_and).then_inc(s_src, 1)
                    if mx:
                        ck.wait(m7)
                        m8 = ck.mark(v.tensor_tensor(rem2[:], rem[:], part[1], ALU.subtract))
                    ck.wait(u1)
                    if has(i, u + FETCH - 2):
                        v.wait_ge(s_oh, c + FETCH - 1)
                    v.tensor_copy(lo_f[:, (u + FETCH) % 2, :], lo_i[:]).then_inc(s_lo, 1)
                    if mx:
                        ck.wait(m8)
                        v.tensor_copy(part[2], rem2[:]).then_inc(s_max, 1)
                        ck.mark(v.tensor_tensor(pk, pk, leak[:], ALU.max))
                    if wg:
                        v.wait_ge(s_wgt, c + WEIGH + 1)
                        mg = msg[:, (u + WEIGH) % MS]
                        v.tensor_tensor(mg[:, :, :, 0:EXP],
                                        got[:, xw, :, 0:H16].rearrange("p t (h e) -> p t h e", e=EXP),
                                        mg[:, :, :, EXP:EXP + 1].to_broadcast([P, EC, HEADS, EXP]),
                                        ALU.mult).then_inc(s_msg, 1)
                    v.wait_ge(s_lo, c + FETCH + 1)

                v.wait_ge(s_sel, 5)
                ck = Chain(v, s_gch, 0)
                for d in range(-FETCH, 0):
                    step(0, d, ck)
                hand_on(0)
                pre, per = ck.n, SL * 14
                with v.Fori(0, rounds(v)) as i:
                    ck = Chain(v, s_gch, pre + per * i)
                    take_over()
                    for d in range(SL):
                        step(i, d, ck)
                    ck.end(per)
                    hand_on(SL)

            @block.scalar
            def _(s):
                def parts(i, d):
                    s.wait_ge(s_stp, SL * i + d + 1)
                    s.wait_ge(s_bc, SL * i + d)
                    s.activation(split[:], split_ps[0:NSP, 0:CE], ACT.Copy).then_inc(s_spl, 1)

                def weights(i, d):
                    s.wait_ge(s_q, SL * i + d + 1)
                    s.activation(msg[:, d % MS, :, :, EXP:EXP + 1].rearrange("p t h o -> p t (h o)"), zq[:],
                                 ACT.Exp).then_inc(s_wgt, 1)

                def transposed(i, d):
                    s.wait_ge(s_otp, SL * i + d + 1)
                    s.activation(pickT[:, d % TS, :], pickT_ps[:], ACT.Copy)
                    s.activation(away[:, d % TS, :], pickT_ps[:], ACT.Identity, bias=far_b[:, 0:1],
                                 scale=BIG).then_inc(s_ot, 1)

                def rescale(i, d):
                    s.wait_ge(s_max, SL * i + d + 1)
                    s.activation(resc[:, d % RS, :], fall[:], ACT.Exp).then_inc(s_resc, 1)

                def one_hot(i, d):
                    s.wait_ge(s_lo, SL * i + d + 1)
                    s.wait_ge(s_oh, SL * i + d)
                    for t in range(EC):
                        last = s.activation(apart[:, t, :], iota_b[:], ACT.Square,
                                            bias=lo_f[:, d % 2, t:t + 1], scale=-1.0)
                    last.then_inc(s_far, 1)
                    s.wait_ge(s_far, SL * i + d + 1)
                    s.activation(pick[:, d % SL], apart[:], ACT.Relu, bias=ones[:, 0:1],
                                 scale=-1.0).then_inc(s_oh, 1)

                def step(i, d):
                    if has(i, d + SPREAD):
                        parts(i, d + SPREAD)
                    if has(i, d + WEIGH):
                        weights(i, d + WEIGH)
                    if has(i, d + SPREAD):
                        transposed(i, d + SPREAD)
                    if has(i, d + MAX):
                        rescale(i, d + MAX)
                    one_hot(i, d + FETCH)

                s.wait_ge(s_sel, 5)
                run(s, step)

            @block.tensor
            def _(t):
                def node_values(i, d):
                    t.wait_ge(s_max, SL * i + d + 1)
                    t.wait_ge(s_q, SL * i + d)
                    for k in range(EC):
                        last = t.matmul(node_v[:, k, :], pickT[:, d % TS, k * P:(k + 1) * P],
                                        node_b[:, d % 2].rearrange("p k f -> p (k f)"),
                                        start=True, stop=True)
                    last.then_inc(s_pg, 1)

                def transpose_parts(i, d):
                    t.wait_ge(s_gat[d % SL], 16 * EC * (i + d // SL) + 16 * EC)
                    t.wait_ge(s_spl, SL * i + d)
                    for k in range(EC):
                        parts_ = got[:, d % SL, k, SPLIT // 2:SPLIT // 2 + NSP // 2].bitcast(BF16)
                        last = t.transpose(split_ps[0:NSP, k * P:(k + 1) * P], parts_, ident_b[:])
                    last.then_inc(s_stp, 1)

                def scatter(i, d):
                    t.wait_ge(s_msg, SL * i + d + 1)
                    t.wait_ge(s_sum, SL * i + d)
                    for k in range(EC):
                        last = t.matmul(sum_v, pick[:, d % SL, k, :],
                                        msg[:, d % MS, k].rearrange("p h e -> p (h e)"),
                                        start=(k == 0), stop=(k == EC - 1))
                    last.then_inc(s_pa2, 1)

                def transpose_pick(i, d):
                    t.wait_ge(s_oh, SL * i + d + 1)
                    t.wait_ge(s_ot, SL * i + d)
                    for k in range(EC):
                        last = t.transpose(pickT_ps[:, k * P:(k + 1) * P], pick[:, d % SL, k, :], ident[:])
                    last.then_inc(s_otp, 1)

                def broadcast(i, d):
                    t.wait_ge(s_spl, SL * i + d + 1)
                    for h in range(HEADS):
                        if has(i, d - 1):
                            t.wait_ge(s_cmax, HEADS * (SL * i + d - 1) + h + 1)
                        last = t.matmul(bc_ps[:, h, :], sel3[:, h, :], split[:], start=True, stop=True)
                    last.then_inc(s_bc, 1)

                def step(i, d):
                    if has(i, d + WEIGH):
                        node_values(i, d + WEIGH)
                    if has(i, d + SPREAD):
                        transpose_parts(i, d + SPREAD)
                    if has(i, d):
                        scatter(i, d)
                    if has(i, d + SPREAD):
                        transpose_pick(i, d + SPREAD)
                        broadcast(i, d + SPREAD)

                t.wait_ge(s_sel, 5)
                run(t, step)

        gates = sb("gates", [P, BINS, EXP], F32)
        s_nw = sem("s_nw")
        s_nch = sem("s_nch")
        s_nv = sem("s_nv")
        s_na = sem("s_na")
        with ExitStack() as st, nc.Block() as block:
            agg = sb("agg", [P, BINS, HEADS, EXP], F32, st)
            agg2 = sb("agg2", [P, BINS, H16], F32, st)
            rec = sb("rec", [P, BINS, HEADS], F32, st)
            vec = [sb(f"vec{i}", [P, BINS], F32, st) for i in range(3)]
            rank = sb("rank", [P, BINS, EXP], F32, st)
            beats = sb("beats", [P, BINS], F32, st)
            score = sb("score", [P, BINS, EXP], F32, st)
            e_score = sb("e_score", [P, BINS, EXP], F32, st)
            params = sb("params", [P, 3, H16], F32, st)
            agg_f = agg[:].rearrange("p n h e -> p n (h e)")
            wide = [P, BINS, H16]

            @block.sync
            def _(sp):
                for i, name in enumerate(("b_gat", "ln_gamma", "ln_beta")):
                    sp.dma_start(params[:, i, :], a[name].rearrange("(o n) -> o n", o=1).partition_broadcast(P)
                                 .rearrange("p o n -> p (o n)")).then_inc(s_nw, 16)

            @block.scalar
            def _(s):
                s.wait_ge(s_nv, 1)
                s.activation(vec[1][:], vec[0][:], ACT.Sqrt, bias=eps5[:, 0:1], scale=1.0 / H16).then_inc(s_na, 1)
                s.wait_ge(s_nv, 2)
                s.activation(e_score[:], rank[:], ACT.Exp).then_inc(s_na, 1)

            @block.vector
            def _(v):
                ck = Chain(v, s_nch)

                def spread(x, n):
                    return x.unsqueeze(2).to_broadcast([P, BINS, n])

                def param(i):
                    return params[:, i, :].unsqueeze(1).to_broadcast(wide)

                ck(v.tensor_scalar(rec[:], total[:, :, :, EXP:EXP + 1].rearrange("p n h o -> p n (h o)"), 1e-16, None,
                                   ALU.add))
                ck(v.reciprocal(rec[:], rec[:]))
                for h in range(HEADS):
                    op = v.tensor_tensor(agg[:, :, h, :], total[:, :, h, 0:EXP], spread(rec[:, :, h], EXP), ALU.mult)
                ck(op)
                v.wait_ge(s_nw, 48)
                ck(v.tensor_tensor(agg_f, agg_f, param(0), ALU.add))
                ck(v.tensor_reduce(vec[0][:], agg_f, AX.X, ALU.add))
                ck(v.tensor_scalar(vec[0][:], vec[0][:], 1.0 / H16, None, ALU.mult))
                ck(v.tensor_tensor(agg_f, agg_f, spread(vec[0][:], H16), ALU.subtract))
                ck(v.tensor_tensor(agg2[:], agg_f, agg_f, ALU.mult))
                ck(v.tensor_reduce(vec[0][:], agg2[:], AX.X, ALU.add))
                v.sem_inc(s_nv, 1)
                v.wait_ge(s_na, 1)
                ck(v.reciprocal(vec[2][:], vec[1][:]))
                ck(v.tensor_tensor(agg_f, agg_f, spread(vec[2][:], H16), ALU.mult))
                ck(v.tensor_tensor(agg_f, agg_f, param(1), ALU.mult))
                ck(v.tensor_tensor(agg_f, agg_f, param(2), ALU.add))
                ck(v.tensor_reduce(score[:], agg[:].rearrange("p n h e -> p n e h"), AX.X, ALU.add))
                ck(v.tensor_scalar(score[:], score[:], 1.0 / HEADS, None, ALU.mult))
                ck(v.memset(rank[:], 0.0))
                for i in range(EXP):
                    for j in range(EXP):
                        if i != j:
                            ck(v.tensor_tensor(beats[:], score[:, :, j], score[:, :, i],
                                               ALU.is_ge if j < i else ALU.is_gt))
                            ck(v.tensor_tensor(rank[:, :, i], rank[:, :, i], beats[:], ALU.add))
                ck(v.tensor_scalar(gates[:], rank[:], 2.0, None, ALU.is_lt))
                ck(v.tensor_reduce(vec[0][:], score[:], AX.X, ALU.max))
                ck(v.tensor_tensor(rank[:], score[:], spread(vec[0][:], EXP), ALU.subtract))
                v.sem_inc(s_nv, 1)
                v.wait_ge(s_na, 2)
                ck(v.tensor_tensor(gates[:], gates[:], e_score[:], ALU.mult))
                ck(v.tensor_reduce(vec[0][:], gates[:], AX.X, ALU.add))
                ck(v.reciprocal(vec[1][:], vec[0][:]))
                ck(v.tensor_tensor(gates[:], gates[:], spread(vec[1][:], EXP), ALU.mult))

        s_mw = sem("s_mw")
        s_g4 = sem("s_g4")
        s_gtp = sem("s_gtp")
        s_gt = sem("s_gt")
        s_gb2 = sem("s_gb2")
        s_hid = sem("s_hid")
        s_gelu = sem("s_gelu")
        s_hg = sem("s_hg")
        s_used = sem("s_used")
        s_po = sem("s_po")
        s_fin = sem("s_fin")
        s_out = [sem("s_out0"), sem("s_out1")]
        with ExitStack() as st, nc.Block() as block:
            w1 = sb("w1", [P, EXP, D2], F32, st)
            w2 = sb("w2", [P, EXP, FH, P], F32, st)
            b1 = sb("b1", [P, EXP, FH], F32, st)
            b2 = sb("b2", [EXP, P], F32, st)
            g4 = sb("g4", [P, 4, EXP], F32, st)
            gT = sb("gT", [EXP, QW], F32, st)
            hid = sb("hid", [P, 2, QW], F32, st)
            hg = sb("hg", [P, 2, QW], F32, st)
            ost = sb("ost", [P, 2, QW], F32, st)
            hid_ps = ps("hid_ps", [P, 2, QW], F32, st)
            gate_ps = ps("gate_ps", [P, 2, QW], F32, st)
            out_ps = ps("out_ps", [P, QW], F32, st)
            gT_ps = ps("gT_ps", [P, QW], F32, st)
            U = EXP * FH
            out = a["out"].rearrange("b c h w -> b c (h w)")

            @block.sync
            def _(sp):
                sp.dma_start(w1[:], a["W1"].rearrange("e d f -> d e f")).then_inc(s_mw, 16)
                sp.dma_start(w2[:], a["W2"].rearrange("e (f p) d -> p e f d", p=P)).then_inc(s_mw, 16)
                with nc.allow_non_contiguous_dma(reason="small parameters, one to a partition"):
                    sp.dma_start(b1[:], a["b1"].rearrange("e (f p) -> p e f", p=P)).then_inc(s_mw, 16)
                sp.dma_start(b2[:], a["b2"]).then_inc(s_mw, 16)
                with sp.Fori(0, B) as b:
                    for h in range(HALF):
                        sp.wait_ge(s_fin, 2 * b + h + 1)
                        sp.dma_start(out[bass.ds(b, 1), :, h * QW:(h + 1) * QW].rearrange("o c s -> (o c) s"),
                                     ost[:, h, :]).then_inc(s_out[h], 16)
                for h in range(HALF):
                    sp.wait_ge(s_out[h], 16 * B)

            @block.scalar
            def _(s):
                s.wait_ge(s_mw, 64)
                with s.Fori(0, B) as b:
                    for h in range(HALF):
                        g = 2 * b + h
                        wait_apart(s, (s_gtp, g))
                        s.activation(g4[:], gates[:, bass.ds(g * 4, 4), :], ACT.Copy).then_inc(s_g4, 1)
                        s.wait_ge(s_gtp, g + 1)
                        s.wait_ge(s_used, U * g)
                        s.activation(gT[:], gT_ps[0:EXP, :], ACT.Copy).then_inc(s_gt, 1)
                        for u in range(U):
                            s.wait_ge(s_hid, U * g + u + 1)
                            if u >= 2:
                                s.wait_ge(s_hg, U * g + u - 1)
                            else:
                                s.wait_ge(s_hg, U * g)
                            s.activation(hid[:, u % 2, :], hid_ps[:, u % 2, :], ACT.Gelu,
                                         bias=b1[:, u // FH, u % FH:u % FH + 1]).then_inc(s_gelu, 1)

            @block.vector
            def _(v):
                with v.Fori(0, B) as b:
                    for h in range(HALF):
                        g = 2 * b + h
                        for u in range(U):
                            v.wait_ge(s_gelu, U * g + u + 1)
                            v.wait_ge(s_gb2, EXP * g + u // FH + 1)
                            if u >= 2:
                                v.wait_ge(s_used, U * g + u - 1)
                            else:
                                v.wait_ge(s_used, U * g)
                            v.tensor_tensor(hg[:, u % 2, :], hid[:, u % 2, :], gate_ps[:, (u // FH) % 2, :],
                                            ALU.mult).then_inc(s_hg, 1)
                        v.wait_ge(s_po, g + 1)
                        v.wait_ge(s_out[h], 16 * b)
                        v.tensor_tensor(ost[:, h, :], out_ps[:], x2[:, bass.ds(g * QW, QW)],
                                        ALU.add).then_inc(s_fin, 1)

            @block.tensor
            def _(t):
                t.wait_ge(s_mw, 64)
                with t.Fori(0, B) as b:
                    for h in range(HALF):
                        g = 2 * b + h

                        def hidden(u):
                            t.wait_ge(s_gelu, U * g + u - 1 if u >= 2 else U * g)
                            t.matmul(hid_ps[:, u % 2, :], w1[:, u // FH, (u % FH) * P:(u % FH + 1) * P],
                                     tokens[:, bass.ds(g * QW, QW)], start=True, stop=True).then_inc(s_hid, 1)

                        def gate(e):
                            t.wait_ge(s_hg, U * g + FH * (e - 1) if e >= 2 else U * g)
                            t.matmul(gate_ps[:, e % 2, :], ident[0:EXP, e:e + 1].to_broadcast([EXP, P]), gT[:],
                                     start=True, stop=True).then_inc(s_gb2, 1)

                        def project(u):
                            t.wait_ge(s_hg, U * g + u + 1)
                            op = t.matmul(out_ps[:], w2[:, u // FH, u % FH, :], hg[:, u % 2, :],
                                          start=False, stop=(u == U - 1))
                            op.then_inc(s_used, 1)

                        t.wait_ge(s_g4, g + 1)
                        t.wait_ge(s_gt, g)
                        for k in range(4):
                            last = t.transpose(gT_ps[0:EXP, k * P:(k + 1) * P], g4[:, k, :], ident[:])
                        last.then_inc(s_gtp, 1)
                        hidden(0)
                        t.wait_ge(s_gt, g + 1)
                        gate(0)
                        t.wait_ge(s_fin, g)
                        t.matmul(out_ps[:], b2[:], gT[:], start=True, stop=False)
                        for u in range(U):
                            if u + 1 < U:
                                hidden(u + 1)
                            if u % FH == 0 and u // FH + 1 < EXP:
                                gate(u // FH + 1)
                            project(u)
                        t.wait_ge(s_used, U * g + U)
                        t.sem_inc(s_po, 1)




SCRATCH = (("slots", (SLOTS, 1), I32), ("counts", (CH, P), F32), ("bins", (1, CHUNKS + 1), I32),
           ("r", (B, C, S), F32), ("sz", (KC, P, NT), F32), ("tab", (M + 1, ROW), F32))


def layouts(inputs):
    import numpy as np

    def t(name):
        return np.ascontiguousarray(np.asarray(inputs[name]).T)

    c, f = "L0_conv_", "L0_ffn_"
    got = {"x": inputs["x"], "edges": inputs[f + "edge_index"]}
    for m in ("m1_", "m2_"):
        for k in ("Win", "Wx", "Wdt", "Wout"):
            got[m + k + "T"] = t(c + m + k)
        for k in ("convw", "convb", "bdt", "Alog", "D"):
            got[m + k] = inputs[c + m + k]
    for k in ("ln1_g", "ln1_b", "ln2_g", "ln2_b", "b_spa"):
        got[k] = inputs[c + k]
    for k in ("W_mid", "W_spa", "W_res"):
        got[k.lower() + "T"] = t(c + k)
    for k in ("W_gat", "att_src", "att_dst", "b_gat", "ln_gamma", "ln_beta", "W1", "b1", "W2", "b2"):
        got[k] = inputs[f + k]
    return {k: np.ascontiguousarray(v) for k, v in got.items()}


def kernel(**inputs):
    from concourse import bacc
    from concourse.bass_utils import run_bass_kernel_spmd

    nc = bacc.Bacc("TRN2", target_bir_lowering=False, num_devices=1)
    arrays, aps = {}, {}
    for name, array in layouts(inputs).items():
        arrays["in_" + name] = array
        aps[name] = nc.dram_tensor("in_" + name, array.shape, mybir.dt.from_np(array.dtype), kind="ExternalInput").ap()
    aps["scratch"] = {name: nc.dram_tensor("scratch_" + name, shape, dt, kind="Internal").ap()
                      for name, shape, dt in SCRATCH}
    aps["out"] = nc.dram_tensor("out", (B, C, 32, 32), F32, kind="ExternalOutput").ap()
    program(nc, aps)
    return run_bass_kernel_spmd(nc, [arrays], core_ids=[0]).results[0]["out"]
```
